# Optimizing a Trainium2 kernel written in Bass

```python
import numpy as np
import jax
import jax.numpy as jnp

def _softmax(x, axis=-1):
    return jax.nn.softmax(x, axis=axis)

def _gelu(x):
    return jax.nn.gelu(x, approximate=True)

def _silu(x):
    return jax.nn.silu(x)

def _sigmoid(x):
    return jax.nn.sigmoid(x)

def _layernorm(x, axis=-1, eps=1e-05):
    m = jnp.mean(x, axis=axis, keepdims=True)
    v = jnp.var(x, axis=axis, keepdims=True)
    return (x - m) / jnp.sqrt(v + eps)

def _scatter_add(tgt, idx, src, axis=0):
    return tgt.at[idx].add(src)

def _segment_sum(src, seg, n):
    return jax.ops.segment_sum(src, seg, n)
kernel_name = 'mk_adj_resnorm_d1_adj_r2_74aac1'

def setup_inputs(seed: int=0):
    np.random.seed(seed)
    _w = jnp.asarray

    def _rec_inputs():
        import jax
        import jax.numpy as jnp
        _gk = jax.random.key(seed)
        x = -9.806e-05 + 1 * jax.random.normal(jax.random.fold_in(_gk, 1), (8192, 128), jnp.float32)
        _w = (1.0 + jnp.arange(8192, dtype=jnp.float32)) ** (-0.5)
        _w = _w / _w.mean()
        _pij = jnp.clip(0.000244141 * _w[:, None] * _w[None, :], 0.0, 1.0)
        _a = jax.random.uniform(jax.random.fold_in(_gk, 2), (8192, 8192)) < _pij
        _a = jnp.logical_or(_a, jnp.eye(8192, dtype=bool))
        _af = _a.astype(jnp.float32)
        _af = _af * jax.random.uniform(jax.random.fold_in(_gk, 3), (8192, 8192), jnp.float32, 0.05, 1)
        adj = _af
        return (x, adj)
    x, adj = _rec_inputs()

    def _L0_gnn_setup():
        import jax, jax.numpy as jnp
        import numpy as np

        def _lap_mul(A, x):
            d = 1.0 / jnp.sqrt(jnp.sum(A, axis=-1))
            return d[:, None] * (A @ (d[:, None] * x))
        key = jax.random.key(seed)
        k1, k2, k3, k4, k5, k6 = jax.random.split(key, 6)
        N, D_IN, D_OUT = (2048, 128, 128)
        x = jax.random.normal(k1, (N, D_IN), dtype=jnp.float32)
        A = jax.random.uniform(k2, (N, N), dtype=jnp.float32)
        s1 = 1.0 / np.sqrt(D_IN)
        W1 = jax.random.uniform(k3, (D_IN, D_OUT), minval=-s1, maxval=s1, dtype=jnp.float32)
        b1 = jax.random.uniform(k4, (D_OUT,), minval=-s1, maxval=s1, dtype=jnp.float32)
        W2 = jax.random.uniform(k5, (D_IN, D_OUT), minval=-s1, maxval=s1, dtype=jnp.float32)
        b2 = jax.random.uniform(k6, (D_OUT,), minval=-s1, maxval=s1, dtype=jnp.float32)
        return {'x': x, 'A': A, 'W1': W1, 'b1': b1, 'W2': W2, 'b2': b2, 'sigma': 1, 'k': 4}
    _L0_gnn_all = _L0_gnn_setup()
    _L0_gnn_in = {k: v for k, v in _L0_gnn_all.items() if k in ('W1', 'b1', 'W2', 'b2')}
    del _L0_gnn_all
    return {'x': x, 'adj': adj, 'L0_gnn_W1': _L0_gnn_in['W1'], 'L0_gnn_b1': _L0_gnn_in['b1'], 'L0_gnn_W2': _L0_gnn_in['W2'], 'L0_gnn_b2': _L0_gnn_in['b2']}

def reference(x, adj, L0_gnn_W1, L0_gnn_b1, L0_gnn_W2, L0_gnn_b2):
    import jax
    import jax.numpy as jnp

    def _L0_gnn_ref(x, A, W1, b1, W2, b2, sigma, k):
        import jax, jax.numpy as jnp
        import numpy as np

        def _lap_mul(A, x):
            d = 1.0 / jnp.sqrt(jnp.sum(A, axis=-1))
            return d[:, None] * (A @ (d[:, None] * x))
        z = _lap_mul(A, x) @ W1 + b1
        z = jax.nn.leaky_relu(z, negative_slope=0.1)
        sq = jnp.sum(z * z, axis=-1)
        d2 = sq[:, None] + sq[None, :] - 2.0 * (z @ z.T)
        d2 = jnp.maximum(d2, 0.0)
        S = jnp.sqrt(d2 + 1e-10)
        S = jnp.exp(-S / (2.0 * sigma))
        order = jnp.argsort(-S, axis=-1)
        ranks = jnp.argsort(order, axis=-1)
        S = jnp.where(ranks < k, S, 0.0)
        A2 = S + A
        out = _lap_mul(A2, x) @ W2 + b2
        return out
    x = _layernorm(x + _L0_gnn_ref(x, adj, L0_gnn_W1, L0_gnn_b1, L0_gnn_W2, L0_gnn_b2, 1, 4), axis=-1)
    return x

_drawn_inputs = setup_inputs


def setup_inputs(seed=0):
    import zlib

    import numpy as np

    out = dict(_drawn_inputs(seed))
    spreads = {}
    factors = {}
    for name, (base, spread) in spreads.items():
        noise = np.random.default_rng([zlib.crc32(name.encode()), seed]).standard_normal(out[name].shape)
        drawn = base * np.exp(spread * noise) if base else spread * noise
        out[name] = jnp.asarray(drawn.astype(out[name].dtype))
    for name, factor in factors.items():
        out[name] = (out[name] * factor).astype(out[name].dtype)
    return out
```

```python
import concourse.bass as bass
from concourse import mybir
from contextlib import ExitStack



def resnorm_graph_kernel(nc, x_in, adj_in, w1_in, b1_in, w2_in, b2_in, out):
    fp32 = mybir.dt.float32
    bf16 = mybir.dt.bfloat16
    u32 = mybir.dt.uint32
    ALU = mybir.AluOpType
    ACT = mybir.ActivationFunctionType
    X = mybir.AxisListType.X
    ds = bass.ds

    P = 128

    N = P * (x_in.shape[1] // P)
    BLOCKS = N // P
    SB = adj_in.shape[2] // 4
    SUPERS = N // SB
    PER = SB // P
    HALF = PER // 2
    HCOLS = HALF * SB
    BANK = 512
    K = 4
    EPS_DIST, EPS_NORM = 1e-10, 1e-5
    F = P
    LAG = PER + 2

    def tri(i):
        return i * (i + 1) // 2

    LOW = tri(SUPERS)
    HIGH = LOW - SUPERS
    TILES1 = SUPERS * SUPERS
    PROD2 = LOW + HIGH
    TILE_OF = TILES1 - LOW

    def upper_tile(ii, gg):
        return ii * (SUPERS - 1) + gg - 1

    def lower_tile(ii, gg):
        return ii * (SUPERS - 1) + gg + (SUPERS - 1)

    def low_product(ii, gg):
        return tri(ii) + gg, (ii - 1) * (ii + 2) // 2 + gg, ii * (ii + 1) + gg * 2

    def high_product(k, j):
        return numbered((k - 1) * k // 2 + j + LOW)

    def high_column(k, j):
        return (j + down(k) + 1).with_bounds(min_val=0, max_val=SUPERS - 1)

    def numbered(m):
        return m, m - 1, m * 2

    def down(k):
        return k * -1 + (SUPERS - 1) if not isinstance(k, int) else SUPERS - 1 - k

    d_row = nc.dram_tensor("d_row", (BLOCKS, P), fp32).ap()
    sq_rows = nc.dram_tensor("sq_rows", (3, BLOCKS, P), bf16).ap()
    y2_rows = nc.dram_tensor("y2_rows", (N, F), fp32).ap()

    ctx = ExitStack()
    with ctx:
        def sb(name, shape, dt=fp32):
            return ctx.enter_context(nc.sbuf_tensor(name, shape, dt))

        def sem(name):
            return ctx.enter_context(nc.semaphore(name))

        ring = sb("ring", [P, 4 * HCOLS])
        buf_a = sb("buf_a", [P, N])
        buf_b = sb("buf_b", [P, N])
        z_t = sb("z_t", [P, N])
        work = [sb(f"work{i}", [P, SB]) for i in range(6)]
        y_stage = sb("y_stage", [P, 2, HALF * F])
        z_stage = sb("z_stage", [P, 2, P])
        neg_half_sq = sb("neg_half_sq", [P, N // 4], bf16)
        ident = sb("ident", [P, P])
        ones = sb("ones", [P, 1])
        ones_bf = sb("ones_bf", [P, P], bf16)
        w1 = sb("w1", [F, F])
        w2 = sb("w2", [F, F])
        b1 = sb("b1", [F, 1])
        b2 = sb("b2", [P, F])
        row_sum = sb("row_sum", [P, BLOCKS])
        d1 = sb("d1", [P, BLOCKS])
        d2 = sb("d2", [P, BLOCKS])
        sq = sb("sq", [P, BLOCKS])
        best = sb("best", [P, BLOCKS, K])
        sim = sb("sim", [P, BLOCKS, K])
        near = sb("near", [P, BLOCKS, K], u32)
        small = sb("small", [P, 4, PER])
        dist = sb("dist", [P, 2, PER, K])
        top = sb("top", [P, 2, 8])
        top_at = sb("top_at", [P, 2, 8], u32)
        rows_t = sb("rows_t", [BLOCKS, 4, P])
        rows_bf = sb("rows_bf", [BLOCKS, 3, P], bf16)
        gate = sb("gate", [P, 1])
        stat = sb("stat", [P, 4, PER])

        y1 = buf_a
        conv1_t = buf_b
        conv2_t = ring[:, 2 * HCOLS:2 * HCOLS + N]
        partial, acc = work[0:2], work[2]
        lap_t, pre_z, z_sq, d_bcast = work[0], work[1], work[2], work[3]
        y2, x_group = work[0], work[1]
        scores = [buf_a, buf_b]
        near_sum, total_t, row_out, row_sq = work[0], work[1], work[2], work[3]
        x_res = work[4:6]

        prod_ps = ctx.enter_context(nc.psum_tensor("prod_ps", [P, 2 * SB], fp32))
        score_ps = ctx.enter_context(nc.psum_tensor("score_ps", [P, 2 * SB], fp32))
        sums_ps = score_ps[:, 0:PER]
        z_ps = score_ps[:, SB:2 * SB]
        rows_ps = score_ps[0:BLOCKS, BANK:BANK + P]
        turned_ps = score_ps[:, 0:SB]
        dense_ps = score_ps[:, SB:2 * SB]

        s_const = sem("const_landed")
        s_x = sem("x_landed")
        s_memset = sem("constants_set")
        s_zeroed = sem("conv_zeroed")
        s_tile = [sem("tile_half0_landed"), sem("tile_half1_landed")]
        s_prod_half = sem("product_halves_done")
        s_staged = sem("y_halves_staged")
        s_added = sem("products_added")
        s_partial = sem("partial_sums_ready")
        s_acc = sem("partial_sums_added")
        s_sums = sem("row_sums_in_psum")
        s_sums_c = sem("row_sums_copied")
        s_root = sem("roots_ready")
        s_d = sem("d_steps")
        s_y1 = sem("y1_supers_ready")
        s_dall = sem("d1_transposed")
        s_drows = sem("d_rows_copied")
        s_dstored = sem("d_row_stored")
        s_dbc = sem("d_broadcast_landed")
        s_lap = sem("lap_ready")
        s_zps = sem("z_in_psum")
        s_prez = sem("pre_z_ready")
        s_z = sem("z_supers_ready")
        s_zsq = sem("z_squares_ready")
        s_sqps = sem("sq_in_psum")
        s_sq = sem("sq_copied")
        s_sqt = sem("sq_transposed")
        s_split = sem("sq_split_steps")
        s_sqst = sem("sq_rows_stored")
        s_sqld = sem("sq_rows_landed")
        s_zst = sem("z_blocks_staged")
        s_chunk = sem("score_chunks_in_psum")
        s_evac = sem("score_chunks_copied")
        s_top = sem("tops_ready")
        s_at = sem("tops_located")
        s_kept = sem("tops_kept")
        s_dist = sem("distance_steps")
        s_exp = sem("similarity_steps")
        s_deg = sem("degree_steps")
        s_deg_root = sem("degree_roots_ready")
        s_y2 = sem("y2_supers_ready")
        s_y2st = sem("y2_stored")
        s_xg = sem("x_group_landed")
        s_gath = [sem("gathered_even"), sem("gathered_odd")]
        s_wgt = sem("gathered_weighted")
        s_nsum = sem("near_sums_ready")
        s_turn = sem("near_sums_turned")
        s_tot = sem("totals_ready")
        s_dense = sem("dense_in_psum")
        s_norm = sem("norm_steps")
        s_var = sem("variances_summed")
        s_nroot = sem("norm_roots_ready")
        s_done = sem("rows_done")
        s_xres = [sem("x_res_even"), sem("x_res_odd")]
        s_out = sem("out_stored")

        b2_row = b2_in.rearrange("(a f) -> a f", a=1)
        block = ctx.enter_context(nc.Block())

        @block.sync
        def _(sp):
            sp.dma_start(buf_a[:, :], x_in).then_inc(s_x, 16)

            def load(tile, ii, gg, slot, free):
                for h in range(2):
                    for s, v in free(h):
                        sp.wait_ge(s, v)
                    if not (isinstance(tile, int) and tile == 0):
                        sp.wait_ge(s_tile[h], tile * 16)
                    sp.dma_start(ring[:, ds(slot * (2 * HCOLS) + h * HCOLS, HCOLS)],
                                 adj_in[ds((ii * SUPERS + gg) * 2 + h, 1), :, :].rearrange("a p n -> p (a n)")
                                 ).then_inc(s_tile[h], 16)

            def load1(ii, gg, n, products):
                def free(h):
                    return ([(s_partial, (n - 2) * 2 + h + 1)] if not isinstance(n, int) or n >= 2 else []) + (
                        [(s_prod_half, products * 2)] if products is not None else [])
                load(n, ii, gg, n % 2, free)

            for gg in range(1, SUPERS):
                load1(0, gg, upper_tile(0, gg), None)
            load1(0, 0, lower_tile(0, 0), None)
            with sp.Fori(1, SUPERS - 1) as ii:
                with sp.Fori(0, SUPERS - 1 - ii) as q:
                    gg = (q + ii + 1).with_bounds(min_val=0, max_val=SUPERS - 1)
                    load1(ii, gg, upper_tile(ii, gg),
                          low_product(ii, 0)[1] + (q + SUPERS - 1) // SUPERS)
                load1(ii, 0, lower_tile(ii, 0), tri(ii))
                with sp.Fori(1, ii + 1) as gg:
                    load1(ii, gg, lower_tile(ii, gg), low_product(ii, gg)[1])
            last = SUPERS - 1
            load1(last, 0, lower_tile(last, 0), tri(last))
            with sp.Fori(1, SUPERS) as gg:
                load1(last, gg, lower_tile(last, gg), low_product(last, gg)[1])

            sp.wait_ge(s_drows, 1)
            sp.dma_start(d_row, rows_t[:, 0, :]).then_inc(s_dstored, 16)
            sp.wait_ge(s_dstored, 16)
            d_flat = d_row.rearrange("(s b) p -> s (b p)", b=PER)

            def load_d(k):
                if not isinstance(k, int):
                    sp.wait_ge(s_lap, k)
                sp.dma_start(d_bcast[:, :], d_flat[ds(down(k), 1), :].to_broadcast([P, SB])).then_inc(s_dbc, 16)

            load_d(0)
            with sp.Fori(1, SUPERS) as k:
                load_d(k)
                with sp.Fori(0, k) as j:
                    m = high_product(k, j)[0]
                    load(m + TILE_OF, down(k), high_column(k, j), (m + TILE_OF) % 2,
                         lambda h: [(s_prod_half, m * 2 - 3 + h)])

            sp.wait_ge(s_split, 5)
            sp.dma_start(sq_rows.rearrange("r b p -> b r p"), rows_bf[:, :, :]).then_inc(s_sqst, 16)
            sp.wait_ge(s_sqst, 16)
            sq_flat = sq_rows.rearrange("r (q g b) p -> g r q (b p)", g=4, b=BANK // P)
            for g in range(4):
                sp.dma_start(neg_half_sq[32 * g:32 * g + 3, :].rearrange("r (q c) -> r q c", c=BANK),
                             sq_flat[g]).then_inc(s_sqld, 16)

            with sp.Fori(0, SUPERS) as gg:
                with sp.Fori(0, SUPERS) as ii:
                    m = gg * SUPERS + ii + PROD2
                    load(m + TILE_OF, ii, gg, 0, lambda h: [(s_prod_half, m * 2 - 1 + h)])

            def load_x(g, p):
                sp.dma_start(x_res[p][:, :], x_in[:, ds(g * SB, SB)]).then_inc(s_xres[p], 16)

            def store(g, p):
                sp.wait_ge(s_done, g + 1)
                sp.dma_start(out[:, ds(g * SB, SB)], row_out[:, :]).then_inc(s_out, 16)

            load_x(0, 0)
            load_x(1, 1)
            with sp.Fori(0, SUPERS // 2 - 1) as q:
                for p in range(2):
                    store(q * 2 + p, p)
                    load_x(q * 2 + p + 2, p)
            for p in range(2):
                store(SUPERS - 2 + p, p)
            sp.wait_ge(s_out, 16 * SUPERS)

        @block.gpsimd
        def _(pool):
            pool.dma_start(w1[:, :], w1_in).then_inc(s_const, 16)
            pool.dma_start(w2[:, :], w2_in).then_inc(s_const, 16)
            pool.dma_start(b1[:, :], b1_in.rearrange("(f a) -> f a", a=1)).then_inc(s_const, 16)
            pool.dma_start(b2[:, :], b2_row.to_broadcast([P, F])).then_inc(s_const, 16)
            nc.gpsimd.memset(ident[:, :], 0.0).then_inc(s_memset, 1)
            pool.wait_ge(s_memset, 1)
            nc.gpsimd.affine_select(out=ident[:, :], in_=ident[:, :], compare_op=ALU.not_equal, fill=1.0, base=0,
                                    pattern=[[-1, P]], channel_multiplier=1).then_inc(s_memset, 1)
            nc.gpsimd.memset(ones[:, :], 1.0).then_inc(s_memset, 1)
            nc.gpsimd.memset(ones_bf[:, :], 1.0).then_inc(s_memset, 1)
            nc.gpsimd.memset(buf_b[:, :], 0.0).then_inc(s_zeroed, 1)

            def add_partial(count, h):
                pool.wait_ge(s_partial, count + 1)
                pool.wait_ge(s_acc, count)
                nc.gpsimd.tensor_tensor(acc[:, :], acc[:, :], partial[h][:, :], ALU.add).then_inc(s_acc, 1)

            with pool.Fori(0, SUPERS) as ii:
                pool.wait_ge(s_sums, ii)
                pool.wait_ge(s_partial, ii * (2 * SUPERS) + 2)
                nc.gpsimd.tensor_tensor(acc[:, :], partial[0][:, :], partial[1][:, :], ALU.add).then_inc(s_acc, 2)
                with pool.Fori(1, SUPERS) as k:
                    for h in range(2):
                        add_partial((ii * SUPERS + k) * 2 + h, h)

            pool.wait_ge(s_prod_half, 2 * PROD2)
            nc.gpsimd.memset(conv2_t, 0.0).then_inc(s_zeroed, 1)

            y2_view = y2_rows.rearrange("(s b p) f -> s p b f", b=PER, p=P)

            def load_group(g):
                pool.dma_start(x_group[:, :], x_in[:, ds(g * SB, SB)]).then_inc(s_xg, 16)

            def store_group(g):
                pool.wait_ge(s_y2, g + 1)
                pool.dma_start(y2_view[ds(g, 1), :, :, :].rearrange("a p b f -> p (a b) f"),
                               y2[:, :].rearrange("p (b f) -> p b f", f=F)).then_inc(s_y2st, 16)

            pool.wait_ge(s_sq, SUPERS)
            load_group(0)
            with pool.Fori(0, SUPERS - 1) as g:
                store_group(g)
                load_group(g + 1)
            store_group(SUPERS - 1)

            pool.wait_ge(s_kept, 2 * BLOCKS)
            pool.wait_ge(s_y2st, 16 * SUPERS)
            for g in range(SUPERS):
                if g >= 2:
                    pool.wait_ge(s_nsum, g - 1)
                for j in range(PER * K):
                    nc.gpsimd.indirect_dma_start(
                        scores[g % 2][:, j * F:(j + 1) * F], None, y2_rows,
                        bass.IndirectOffsetOnAxis(ap=near[:, g * PER + j // K, j % K:j % K + 1], axis=0)
                    ).then_inc(s_gath[g % 2], 16)

        @block.scalar
        def _(act):
            def stage_y(product, gg, ready):
                act.wait_ge(s_y1, ready)
                for h in range(2):
                    if not (isinstance(product[0], int) and product[0] == 0):
                        act.wait_ge(s_prod_half, product[2] - 1 + h)
                    nc.scalar.copy(y_stage[:, h, :], y1[:, ds(gg * (PER * F) + h * (HALF * F), HALF * F)]
                                   ).then_inc(s_staged, 1)

            def root(ii):
                act.wait_ge(s_sums_c, ii + 1)
                nc.scalar.activation(small[:, 1, :], small[:, 0, :], ACT.Sqrt).then_inc(s_root, 1)

            root(0)
            stage_y(low_product(0, 0), 0, 1)
            with act.Fori(1, SUPERS) as ii:
                with act.Fori(0, ii) as gg:
                    stage_y(low_product(ii, gg), gg, 1)
                root(ii)
                stage_y(low_product(ii, ii), ii, ii + 1)

            def z_part(k):
                act.wait_ge(s_zps, k + 1)
                nc.scalar.activation(pre_z[:, :], z_ps, ACT.Identity, bias=b1[:, 0:1]).then_inc(s_prez, 1)
                act.wait_ge(s_z, k + 1)
                nc.scalar.activation(z_sq[:, :], z_t[:, ds(down(k) * SB, SB)], ACT.Square).then_inc(s_zsq, 1)

            z_part(0)
            with act.Fori(1, SUPERS) as k:
                with act.Fori(0, k) as j:
                    stage_y(high_product(k, j), high_column(k, j), SUPERS)
                z_part(k)

            def search(t, p, first=False):
                if not first:
                    act.wait_ge(s_chunk, t * PER - PER)
                nc.scalar.copy(z_stage[:, p, :], z_t[:, ds(t * P, P)]).then_inc(s_zst, 1)
                if not first:
                    act.wait_ge(s_at, t - 1)
                for c in range(PER):
                    act.wait_ge(s_chunk, t * PER + c + 1)
                    nc.scalar.copy(scores[p][:, c * SB:(c + 1) * SB],
                                   score_ps[:, (c % 2) * SB:(c % 2 + 1) * SB]).then_inc(s_evac, 1)

            def similarities(g):
                act.wait_ge(s_dist, g * 2 + 2)
                nc.scalar.activation(dist[:, 0], dist[:, 0], ACT.Sqrt).then_inc(s_exp, 1)
                act.wait_ge(s_exp, g * 2 + 1)
                nc.scalar.activation(dist[:, 1], dist[:, 0], ACT.Exp, scale=-0.5).then_inc(s_exp, 1)
                act.wait_ge(s_deg, g * 4 + 2)
                nc.scalar.activation(small[:, 1, :], small[:, 0, :], ACT.Sqrt).then_inc(s_deg_root, 1)

            def segment(g):
                with act.Fori(0, PER // 2 - 1) as q:
                    for p in range(2):
                        search(g * PER + q * 2 + 2 + p, p)
                for p in range(2):
                    search(g * PER + PER + p, p)
                similarities(g)

            act.wait_ge(s_sq, SUPERS)
            act.wait_ge(s_prod_half, 2 * PROD2)
            search(0, 0, True)
            search(1, 1, True)
            with act.Fori(0, SUPERS - 1) as g:
                segment(g)
            with act.Fori(0, PER // 2 - 1) as q:
                for p in range(2):
                    search(q * 2 + BLOCKS - PER + 2 + p, p)
            similarities(SUPERS - 1)

            with act.Fori(0, SUPERS) as g:
                act.wait_ge(s_norm, g * 8 + 7)
                nc.scalar.activation(stat[:, 2, :], stat[:, 1, :], ACT.Sqrt).then_inc(s_nroot, 1)

        @block.vector
        def _(dve):
            def sum_tile(n):
                for h in range(2):
                    dve.wait_ge(s_tile[h], n * 16 + 16)
                    if not (isinstance(n, int) and n == 0):
                        dve.wait_ge(s_acc, n * 2 - 1 + h)
                    nc.vector.tensor_reduce(
                        partial[h][:, :],
                        ring[:, ds((n % 2) * (2 * HCOLS) + h * HCOLS, HCOLS)].rearrange("p (b i) -> p i b", b=HALF),
                        X, ALU.add).then_inc(s_partial, 1)

            def add_product(product, target, at):
                m, _, halves = product
                dve.wait_ge(s_prod_half, halves + 2)
                dve.wait_ge(s_added, m)
                nc.vector.tensor_tensor(target[:, ds(at, SB)], target[:, ds(at, SB)],
                                        prod_ps[:, ds((m % 2) * SB, SB)], ALU.add).then_inc(s_added, 1)

            def finish_rows(ii):
                dve.wait_ge(s_sums, ii + 1)
                nc.vector.tensor_copy(small[:, 0, :], sums_ps).then_inc(s_sums_c, 1)
                nc.vector.tensor_copy(row_sum[:, ds(ii * PER, PER)], sums_ps)
                dve.wait_ge(s_root, ii + 1)
                nc.vector.reciprocal(small[:, 2, :], small[:, 1, :]).then_inc(s_d, 1)
                dve.wait_ge(s_d, ii * 2 + 1)
                nc.vector.tensor_copy(d1[:, ds(ii * PER, PER)], small[:, 2, :]).then_inc(s_d, 1)
                v = y1[:, ds(ii * SB, SB)].rearrange("p (b f) -> p b f", f=F)
                nc.vector.tensor_tensor(v, v, small[:, 2, :].unsqueeze(2).to_broadcast([P, PER, F]),
                                        ALU.mult).then_inc(s_y1, 1)

            dve.wait_ge(s_x, 16)
            for n in range(SUPERS):
                sum_tile(n)
            finish_rows(0)
            dve.wait_ge(s_zeroed, 1)
            with dve.Fori(1, SUPERS - 1) as ii:
                with dve.Fori(ii + 1, SUPERS) as gg:
                    sum_tile(upper_tile(ii, gg))
                add_product(low_product(ii - 1, ii - 1), conv1_t, ii * SB - SB)
                sum_tile(lower_tile(ii, 0))
                with dve.Fori(1, ii + 1) as gg:
                    sum_tile(lower_tile(ii, gg))
                    add_product(low_product(ii, gg - 1), conv1_t, ii * SB)
                finish_rows(ii)
            last = SUPERS - 1
            add_product(numbered(tri(last) - 1), conv1_t, last * SB - SB)
            sum_tile(lower_tile(last, 0))
            with dve.Fori(1, SUPERS) as gg:
                sum_tile(lower_tile(last, gg))
                add_product(numbered(gg + (tri(last) - 1)), conv1_t, last * SB)
            finish_rows(last)
            dve.wait_ge(s_dall, 1)
            nc.vector.tensor_copy(rows_t[:, 0, :], rows_ps).then_inc(s_drows, 1)
            add_product(numbered(LOW - 1), conv1_t, last * SB)

            def z_part(k, added):
                dve.wait_ge(s_dbc, k * 16 + 16)
                dve.wait_ge(s_added, added)
                if not isinstance(k, int):
                    dve.wait_ge(s_zps, k)
                nc.vector.tensor_tensor(lap_t[:, :], conv1_t[:, ds(down(k) * SB, SB)], d_bcast[:, :],
                                        ALU.mult).then_inc(s_lap, 1)
                dve.wait_ge(s_prez, k + 1)
                nc.vector.scalar_tensor_tensor(z_t[:, ds(down(k) * SB, SB)], pre_z[:, :], 0.1, pre_z[:, :],
                                               ALU.mult, ALU.max).then_inc(s_z, 1)
                dve.wait_ge(s_sqps, k + 1)
                nc.vector.tensor_copy(sq[:, ds(down(k) * PER, PER)], sums_ps).then_inc(s_sq, 1)

            z_part(0, LOW)
            with dve.Fori(1, SUPERS) as k:
                with dve.Fori(0, k) as j:
                    add_product(high_product(k, j), conv1_t, down(k) * SB)
                z_part(k, high_product(k, k)[0])

            dve.wait_ge(s_sqt, 1)
            nc.vector.tensor_scalar(rows_t[:, 1, :], rows_ps, -0.5, None, ALU.mult).then_inc(s_split, 1)
            dve.wait_ge(s_split, 1)
            nc.vector.tensor_copy(rows_bf[:, 0, :], rows_t[:, 1, :]).then_inc(s_split, 1)
            dve.wait_ge(s_split, 2)
            nc.vector.tensor_tensor(rows_t[:, 2, :], rows_t[:, 1, :], rows_bf[:, 0, :],
                                    ALU.subtract).then_inc(s_split, 1)
            dve.wait_ge(s_split, 3)
            nc.vector.tensor_copy(rows_bf[:, 1, :], rows_t[:, 2, :]).then_inc(s_split, 1)
            dve.wait_ge(s_split, 4)
            nc.vector.tensor_tensor(rows_bf[:, 2, :], rows_t[:, 2, :], rows_bf[:, 1, :],
                                    ALU.subtract).then_inc(s_split, 1)

            def search(t, p):
                dve.wait_ge(s_evac, t * PER + PER)
                nc.vector.tensor_copy(gate[:, 0:1], ones[:, :])
                nc.vector.max(top[:, p, :], scores[p][:, :]).then_inc(s_top, 1)
                dve.wait_ge(s_top, t + 1)
                nc.vector.tensor_copy(best[:, ds(t, 1), :].rearrange("p a k -> p (a k)"),
                                      top[:, p, 0:K]).then_inc(s_kept, 1)
                nc.vector.max_index(top_at[:, p, :], top[:, p, :], scores[p][:, :]).then_inc(s_at, 1)
                dve.wait_ge(s_at, t + 1)
                nc.vector.tensor_copy(near[:, ds(t, 1), :].rearrange("p a k -> p (a k)"),
                                      top_at[:, p, 0:K]).then_inc(s_kept, 1)

            def follow(t):
                u = t - LAG
                add_product(numbered(u + PROD2), conv2_t, (u % SUPERS) * SB)

            def new_degrees(g, kept):
                at = ds(g * PER, PER)
                dve.wait_ge(s_kept, kept)
                nc.vector.scalar_tensor_tensor(dist[:, 0], best[:, at, :], -2.0,
                                               sq[:, at].unsqueeze(2).to_broadcast([P, PER, K]),
                                               ALU.mult, ALU.add).then_inc(s_dist, 1)
                dve.wait_ge(s_dist, g * 2 + 1)
                nc.vector.tensor_scalar(dist[:, 0], dist[:, 0], 0.0, EPS_DIST, ALU.max, ALU.add).then_inc(s_dist, 1)
                dve.wait_ge(s_exp, g * 2 + 2)
                nc.vector.tensor_reduce(small[:, 3, :], dist[:, 1], X, ALU.add).then_inc(s_deg, 1)
                nc.vector.tensor_copy(sim[:, at, :], dist[:, 1])
                dve.wait_ge(s_deg, g * 4 + 1)
                nc.vector.tensor_tensor(small[:, 0, :], small[:, 3, :], row_sum[:, at], ALU.add).then_inc(s_deg, 1)
                dve.wait_ge(s_deg_root, g + 1)
                nc.vector.reciprocal(small[:, 2, :], small[:, 1, :]).then_inc(s_deg, 1)
                dve.wait_ge(s_deg, g * 4 + 3)
                nc.vector.tensor_copy(d2[:, at], small[:, 2, :]).then_inc(s_deg, 1)
                dve.wait_ge(s_xg, g * 16 + 16)
                if not (isinstance(g, int) and g == 0):
                    dve.wait_ge(s_y2st, g * 16)
                dve.wait_ge(s_prod_half, (g * SUPERS + PROD2) * 2)
                nc.vector.tensor_tensor(y2[:, :].rearrange("p (b f) -> p b f", f=F),
                                        x_group[:, :].rearrange("p (b f) -> p b f", f=F),
                                        small[:, 2, :].unsqueeze(2).to_broadcast([P, PER, F]),
                                        ALU.mult).then_inc(s_y2, 1)

            def segment(g, with_products):
                with dve.Fori(0, PER // 2 - 1) as q:
                    for p in range(2):
                        t = g * PER + q * 2 + 2 + p
                        search(t, p)
                        if with_products:
                            follow(t)
                for p in range(2):
                    t = g * PER + PER + p
                    search(t, p)
                    if with_products:
                        follow(t)
                    if p == 0:
                        new_degrees(g, (g * PER + PER + 1) * 2)

            search(0, 0)
            search(1, 1)
            segment(0, False)
            dve.wait_ge(s_zeroed, 2)
            with dve.Fori(1, SUPERS - 1) as g:
                segment(g, True)
            with dve.Fori(0, PER // 2 - 1) as q:
                for p in range(2):
                    t = q * 2 + BLOCKS - PER + 2 + p
                    search(t, p)
                    follow(t)
            new_degrees(SUPERS - 1, 2 * BLOCKS)
            with dve.Fori(BLOCKS, BLOCKS + LAG) as t:
                follow(t)

            def finish(g, q, p):
                at = ds(g * PER, PER)
                gathered = scores[p][:, 0:PER * K * F].rearrange("p (b k f) -> p b k f", k=K, f=F)
                out3 = row_out[:, :].rearrange("p (b f) -> p b f", f=F)
                sq3 = row_sq[:, :].rearrange("p (b f) -> p b f", f=F)
                dve.wait_ge(s_gath[p], (q + 1) * (16 * PER * K))
                for b in range(PER):
                    w = nc.vector.tensor_tensor(
                        gathered[:, b], gathered[:, b],
                        sim[:, ds(g * PER + b, 1), :].rearrange("p a k -> p (a k)").unsqueeze(2).to_broadcast([P, K, F]),
                        ALU.mult)
                w.then_inc(s_wgt, 1)
                dve.wait_ge(s_wgt, g + 1)
                nc.vector.tensor_reduce(near_sum[:, :].rearrange("p (b f) -> p b f", f=F),
                                        gathered.rearrange("p b k f -> p b f k"), X, ALU.add).then_inc(s_nsum, 1)
                dve.wait_ge(s_turn, g + 1)
                nc.vector.tensor_tensor(total_t[:, :], turned_ps, conv2_t[:, ds(g * SB, SB)],
                                        ALU.add).then_inc(s_tot, 1)
                dve.wait_ge(s_dense, g + 1)
                if not (isinstance(g, int) and g == 0):
                    dve.wait_ge(s_out, g * 16)
                n = [0]

                def step(ins):
                    n[0] += 1
                    ins.then_inc(s_norm, 1)
                    dve.wait_ge(s_norm, g * 8 + n[0])

                step(nc.vector.tensor_tensor(out3, dense_ps.rearrange("p (b f) -> p b f", f=F),
                                             d2[:, at].unsqueeze(2).to_broadcast([P, PER, F]), ALU.mult))
                step(nc.vector.tensor_tensor(out3, out3, b2[:, :].unsqueeze(1).to_broadcast([P, PER, F]), ALU.add))
                dve.wait_ge(s_xres[p], q * 16 + 16)
                step(nc.vector.tensor_tensor(row_out[:, :], row_out[:, :], x_res[p][:, :], ALU.add))
                step(nc.vector.tensor_reduce(stat[:, 0, :], out3, X, ALU.add))
                nc.vector.scalar_tensor_tensor(out3, stat[:, 0, :].unsqueeze(2).to_broadcast([P, PER, F]), -1.0 / F,
                                               out3, ALU.mult, ALU.add).then_inc(s_norm, 1)
                dve.wait_ge(s_norm, g * 8 + 5)
                nc.vector.tensor_tensor(row_sq[:, :], row_out[:, :], row_out[:, :], ALU.mult).then_inc(s_norm, 1)
                dve.wait_ge(s_norm, g * 8 + 6)
                nc.vector.tensor_reduce(stat[:, 0, :], sq3, X, ALU.add).then_inc(s_var, 1)
                dve.wait_ge(s_var, g + 1)
                nc.vector.tensor_scalar(stat[:, 1, :], stat[:, 0, :], 1.0 / F, EPS_NORM, ALU.mult,
                                        ALU.add).then_inc(s_norm, 1)
                dve.wait_ge(s_nroot, g + 1)
                nc.vector.reciprocal(stat[:, 3, :], stat[:, 2, :]).then_inc(s_norm, 1)
                dve.wait_ge(s_norm, g * 8 + 8)
                nc.vector.tensor_tensor(out3, out3, stat[:, 3, :].unsqueeze(2).to_broadcast([P, PER, F]),
                                        ALU.mult).then_inc(s_done, 1)


            dve.wait_ge(s_added, PROD2 + BLOCKS)
            for p in range(2):
                finish(p, 0, p)
            with dve.Fori(1, SUPERS // 2) as q:
                for p in range(2):
                    finish(q * 2 + p, q, p)

        @block.tensor
        def _(pe):
            def product(number, tile, slot, stationary, ready):
                m, before, _ = number
                if not (isinstance(m, int) and m < 2):
                    pe.wait_ge(s_added, before)
                for h in range(2):
                    pe.wait_ge(s_tile[h], tile * 16 + 16)
                    for s, v in ready(h):
                        pe.wait_ge(s, v)
                    for b in range(HALF):
                        for c in range(SB // BANK):
                            last = nc.tensor.matmul(
                                prod_ps[:, ds((m % 2) * SB + c * BANK, BANK)], stationary(h, b),
                                ring[:, ds(slot * (2 * HCOLS) + h * HCOLS + b * SB + c * BANK, BANK)],
                                start=(h == 0 and b == 0), stop=(h == 1 and b == HALF - 1))
                    last.then_inc(s_prod_half, 1)

            def product12(number, tile):
                product(number, tile, tile % 2, lambda h, b: y_stage[:, h, b * F:(b + 1) * F],
                        lambda h: [(s_staged, number[2] + h + 1)])

            def row_sums(ii):
                pe.wait_ge(s_acc, ii * (2 * SUPERS) + 2 * SUPERS)
                if not (isinstance(ii, int) and ii == 0):
                    pe.wait_ge(s_d, ii * 2)
                for b in range(PER):
                    last = nc.tensor.matmul(sums_ps[:, b:b + 1], acc[:, b * P:(b + 1) * P], ones[:, :],
                                            start=True, stop=True)
                last.then_inc(s_sums, 1)

            pe.wait_ge(s_memset, 4)
            pe.wait_ge(s_const, 64)
            row_sums(0)
            product12(low_product(0, 0), lower_tile(0, 0))
            with pe.Fori(1, SUPERS) as ii:
                with pe.Fori(0, ii) as gg:
                    product12(low_product(ii, gg), lower_tile(ii, gg))
                row_sums(ii)
                product12(low_product(ii, ii), lower_tile(ii, ii))
            pe.wait_ge(s_d, 2 * SUPERS)
            nc.tensor.matmul(rows_ps, d1[:, :], ident[:, :], start=True, stop=True).then_inc(s_dall, 1)

            def z_part(k):
                pe.wait_ge(s_lap, k + 1)
                if not isinstance(k, int):
                    pe.wait_ge(s_prez, k)
                for c in range(SB // BANK):
                    last = nc.tensor.matmul(z_ps[:, c * BANK:(c + 1) * BANK], w1[:, :],
                                            lap_t[:, c * BANK:(c + 1) * BANK], start=True, stop=True)
                last.then_inc(s_zps, 1)
                pe.wait_ge(s_zsq, k + 1)
                if not isinstance(k, int):
                    pe.wait_ge(s_sq, k)
                for b in range(PER):
                    last = nc.tensor.matmul(sums_ps[:, b:b + 1], z_sq[:, b * P:(b + 1) * P], ones[:, :],
                                            start=True, stop=True)
                last.then_inc(s_sqps, 1)

            z_part(0)
            with pe.Fori(1, SUPERS) as k:
                with pe.Fori(0, k) as j:
                    m = high_product(k, j)
                    product12(m, m[0] + TILE_OF)
                z_part(k)
            pe.wait_ge(s_sq, SUPERS)
            nc.tensor.matmul(rows_ps, sq[:, :], ident[:, :], start=True, stop=True).then_inc(s_sqt, 1)

            def search(t, p, first=False):
                pe.wait_ge(s_zst, t + 1)
                for c in range(PER):
                    if not (first and c < 2):
                        pe.wait_ge(s_evac, t * PER + c - 1)
                    for half in range(SB // BANK):
                        n = c * (SB // BANK) + half
                        grp = 32 * (n % 4)
                        nc.tensor.matmul(score_ps[:, (c % 2) * SB + half * BANK:(c % 2) * SB + (half + 1) * BANK],
                                         ones_bf[grp:grp + 3, :],
                                         neg_half_sq[grp:grp + 3, (n // 4) * BANK:(n // 4 + 1) * BANK],
                                         start=True, stop=False)
                    for half in range(SB // BANK):
                        n = c * (SB // BANK) + half
                        last = nc.tensor.matmul(
                            score_ps[:, (c % 2) * SB + half * BANK:(c % 2) * SB + (half + 1) * BANK],
                            z_stage[:, p, :], z_t[:, n * BANK:(n + 1) * BANK], start=False, stop=True)
                    last.then_inc(s_chunk, 1)

            def follow(t):
                u = t - LAG
                m = u + PROD2
                product(numbered(m), m + TILE_OF, 0, lambda h, b: y2[:, (h * HALF + b) * F:(h * HALF + b + 1) * F],
                        lambda h: [(s_y2, u // SUPERS + 1)] if h == 0 else [])

            pe.wait_ge(s_split, 1)
            pe.wait_ge(s_sqld, 64)
            search(0, 0, True)
            search(1, 1)
            with pe.Fori(1, PER // 2 + 1) as q:
                for p in range(2):
                    search(q * 2 + p, p)
            with pe.Fori(PER // 2 + 1, BLOCKS // 2) as q:
                for p in range(2):
                    search(q * 2 + p, p)
                    follow(q * 2 + p)
            with pe.Fori(BLOCKS, BLOCKS + LAG) as t:
                follow(t)

            with pe.Fori(0, SUPERS) as g:
                pe.wait_ge(s_nsum, g + 1)
                for b in range(PER):
                    last = nc.tensor.matmul(turned_ps[:, b * P:(b + 1) * P], near_sum[:, b * F:(b + 1) * F],
                                            ident[:, :], start=True, stop=True)
                last.then_inc(s_turn, 1)
                pe.wait_ge(s_tot, g + 1)
                for b in range(PER):
                    last = nc.tensor.matmul(dense_ps[:, b * F:(b + 1) * F], total_t[:, b * P:(b + 1) * P],
                                            w2[:, :], start=True, stop=True)
                last.then_inc(s_dense, 1)


def kernel(x, adj, L0_gnn_W1, L0_gnn_b1, L0_gnn_W2, L0_gnn_b2):
    import numpy as np
    import concourse.bacc as bacc
    from concourse import mybir as _mybir
    from concourse.bass_utils import run_bass_kernel_spmd as run

    x, adj = np.asarray(x), np.asarray(adj)
    n, f = x.shape
    p, sb = 128, 1024
    supers, half = n // sb, sb // p // 2
    x_part = np.ascontiguousarray(x.reshape(n // p, p, f).transpose(1, 0, 2)).reshape(p, n // p * f)
    tiles = np.ascontiguousarray(adj.reshape(supers, sb, supers, 2, half, p).transpose(0, 2, 3, 5, 4, 1))
    tiles = tiles.reshape(supers * supers * 2, p, half * sb)
    arrays = {"x_part": x_part, "adj_tiles": tiles, "w1_dram": np.ascontiguousarray(L0_gnn_W1),
              "b1_dram": np.ascontiguousarray(L0_gnn_b1), "w2_dram": np.ascontiguousarray(L0_gnn_W2),
              "b2_dram": np.ascontiguousarray(L0_gnn_b2)}
    nc = bacc.Bacc("TRN2", target_bir_lowering=False, num_devices=1)
    args = [nc.dram_tensor(k, a.shape, _mybir.dt.from_np(a.dtype), kind="ExternalInput").ap()
            for k, a in arrays.items()]
    out = nc.dram_tensor("out", (p, n // p * f), _mybir.dt.float32, kind="ExternalOutput").ap()
    resnorm_graph_kernel(nc, *args, out)
    r = run(nc, [arrays], core_ids=[0])
    got = np.asarray(r.results[0]["out"])
    return np.ascontiguousarray(got.reshape(p, n // p, f).transpose(1, 0, 2)).reshape(n, f)
```

```python
import concourse.bass as bass
from concourse import mybir
from contextlib import ExitStack



def resnorm_graph_kernel(nc, x_in, adj_in, w1_in, b1_in, w2_in, b2_in, out):
    fp32 = mybir.dt.float32
    bf16 = mybir.dt.bfloat16
    u32 = mybir.dt.uint32
    fp32r = mybir.dt.float32r
    ALU = mybir.AluOpType
    ACT = mybir.ActivationFunctionType
    X = mybir.AxisListType.X
    ds = bass.ds

    P = 128

    N = P * (x_in.shape[1] // P)
    BLOCKS = N // P
    SB = adj_in.shape[2] // 4
    SUPERS = N // SB
    PER = SB // P
    HALF = PER // 2
    HCOLS = HALF * SB
    BANK = 512
    K = 4
    EPS_DIST, EPS_NORM = 1e-10, 1e-5
    F = P
    LAG = PER + 2
    EARLY = BLOCKS // (2 * SUPERS)
    LATE = SUPERS - EARLY
    SLOTS = 7

    def tri(i):
        return i * (i + 1) // 2

    LOW = tri(SUPERS)
    HIGH = LOW - SUPERS
    TILES1 = SUPERS * SUPERS
    PROD2 = LOW + HIGH
    TILE_OF = TILES1 - LOW

    def upper_tile(ii, gg):
        return ii * (SUPERS - 1) + gg - 1

    def lower_tile(ii, gg):
        return ii * (SUPERS - 1) + gg + (SUPERS - 1)

    def low_product(ii, gg):
        return tri(ii) + gg, (ii - 1) * (ii + 2) // 2 + gg, ii * (ii + 1) + gg * 2

    def high_product(k, j):
        return numbered((k - 1) * k // 2 + j + LOW)

    def high_half(k, j, h):
        return (k - 1) * k + j * 2 + h

    def high_column(k, j):
        gg = j + down(k) + 1
        return gg if isinstance(gg, int) else gg.with_bounds(min_val=0, max_val=SUPERS - 1)

    def numbered(m):
        return m, m - 1, m * 2

    def down(k):
        return k * -1 + (SUPERS - 1) if not isinstance(k, int) else SUPERS - 1 - k

    d_row = nc.dram_tensor("d_row", (BLOCKS, P), fp32).ap()
    sq_rows = nc.dram_tensor("sq_rows", (3, BLOCKS, P), bf16).ap()
    y2_rows = nc.dram_tensor("y2_rows", (N, F), fp32).ap()

    ctx = ExitStack()
    with ctx:
        def sb(name, shape, dt=fp32):
            return ctx.enter_context(nc.sbuf_tensor(name, shape, dt))

        def sem(name):
            return ctx.enter_context(nc.semaphore(name))

        base = (nc.sbuf_base + 31) // 32 * 32
        WORD, ROWS = 4, N * 4
        arena = sb("arena", [P, 6 * N + 4 * HALF * F])

        def at(name, offset, shape, dt=fp32):
            return nc.alloc_sbuf_tensor_at(name, shape, dt, offset=base + offset)

        A, B, C, D, E = (i * ROWS for i in range(5))
        del arena
        y1 = at("y1", A, [P, N])
        conv1_t = at("conv1_t", B, [P, N])
        ring = at("ring", C + 4 * SB * 4, [P, SLOTS * HCOLS])
        lower_ring = at("lower_ring", C + 4 * SB * WORD, [P, 2 * HCOLS], fp32r)
        whole_ring = at("whole_ring", C + (4 * SB + 2 * HCOLS) * WORD, [P, 3 * HCOLS])
        upper_ring = at("upper_ring", C + (4 * SB + 5 * HCOLS) * WORD, [P, 2 * HCOLS], fp32r)
        works = [at(f"work{i}", C + i * SB * WORD, [P, SB]) for i in range(4)]
        partial, acc = works[0:2], works[2]
        lap_t, pre_z, z_sq, d_bcast = works
        scores = [at("scores_even", A, [P, N]), at("scores_odd", B, [P, N])]
        z_h = at("z_h", C, [P, N], fp32r)
        z_l = at("z_l", D, [P, N], fp32r)
        half_tile = at("half_tile", E, [P, HCOLS])
        y2_now = at("y2_now", E + HCOLS * WORD, [P, SB])
        x_y2 = at("x_y2", E + (HCOLS + SB) * WORD, [P, SB])
        neg_half_sq = at("neg_half_sq", E + (HCOLS + 2 * SB) * WORD, [P, N // 4], bf16)
        z_stage_h = at("z_stage_h", E + (HCOLS + 3 * SB) * WORD, [P, 2, P], fp32r)
        z_stage_l = at("z_stage_l", E + (HCOLS + 3 * SB + 2 * P) * WORD, [P, 2, P], fp32r)
        conv2_t = at("conv2_t", E + ROWS, [P, N])
        y2_late = at("y2_late", A, [P, LATE * SB])
        near_sum, total_t, row_out, row_sq = (
            at(f"late{i}", A + (LATE + i) * SB * WORD, [P, SB]) for i in range(4))
        gathered = [at(f"gathered{i}", B + i * PER * K * F * WORD, [P, PER * K * F]) for i in range(2)]
        late_ring = at("late_ring", C, [P, 2 * 2 * HCOLS])
        y_stage = at("y_stage", 6 * ROWS + SB * WORD, [P, 2, HALF * F])
        y_stage_h = at("y_stage_h", 6 * ROWS + SB * WORD, [P, 2, HALF * F], fp32r)

        def ring_slot(tile, h, start=0, size=HCOLS):
            return ring[:, ds((tile * 2 + h) % SLOTS * HCOLS + start, size)]

        def whole_slot(v):
            return whole_ring[:, ds(v % 3 * HCOLS, HCOLS)]

        def upper_slot(v, start=0, size=HCOLS):
            return upper_ring[:, ds(v % 2 * HCOLS + start, size)]

        def lower_slot(v, start=0, size=HCOLS):
            return lower_ring[:, ds(v % 2 * HCOLS + start, size)]

        x_res = [y_stage[:, :, :].rearrange("p h n -> p (h n)"), x_y2[:, :]]
        y_stage_l = at("y_stage_l", 6 * ROWS, [P, 2, HALF * F], fp32r)
        rows_t = at("rows_t", 6 * ROWS, [BLOCKS, 3, P])
        rows_bf = at("rows_bf", 6 * ROWS + 3 * P * WORD, [BLOCKS, 3, P], bf16)
        ident = sb("ident", [P, P])
        ones = sb("ones", [P, 1])
        ones_bf = sb("ones_bf", [P, P], bf16)
        w1 = sb("w1", [F, F])
        w2 = sb("w2", [F, F])
        b1 = sb("b1", [F, 1])
        b2 = sb("b2", [P, F])
        row_sum = sb("row_sum", [P, BLOCKS])
        d1 = sb("d1", [P, BLOCKS])
        d2 = sb("d2", [P, BLOCKS])
        sq = sb("sq", [P, BLOCKS])
        best = sb("best", [P, BLOCKS, K])
        sim = sb("sim", [P, BLOCKS, K])
        near = sb("near", [P, BLOCKS, K], u32)
        small = sb("small", [P, 4, PER])
        dist = sb("dist", [P, 2, PER, K])
        top = sb("top", [P, 2, 8])
        top_at = sb("top_at", [P, 2, 8], u32)
        gate = sb("gate", [P, 1])
        stat = sb("stat", [P, 4, PER])

        prod_ps = ctx.enter_context(nc.psum_tensor("prod_ps", [P, 2 * SB], fp32))
        score_ps = ctx.enter_context(nc.psum_tensor("score_ps", [P, 2 * SB], fp32))
        sums_ps = score_ps[:, 0:PER]
        z_ps = score_ps[:, SB:2 * SB]
        rows_ps = score_ps[0:BLOCKS, BANK:BANK + P]
        turned_ps = score_ps[:, 0:SB]
        dense_ps = score_ps[:, SB:2 * SB]

        s_const = sem("const_landed")
        s_x = sem("x_landed")
        s_memset = sem("constants_set")
        s_zeroed = sem("conv_zeroed")
        s_tile = [sem("tile_half0_landed"), sem("tile_half1_landed")]
        s_prod_half = sem("product_halves_done")
        s_staged = sem("y_halves_staged")
        s_added = sem("products_added")
        s_upper = sem("upper_halves_ready")
        s_upper_used = sem("upper_halves_multiplied")
        s_lower = sem("lower_halves_ready")
        s_ylow = sem("y_lower_halves_staged")
        s_partial = sem("partial_sums_ready")
        s_acc = sem("partial_sums_added")
        s_sums = sem("row_sums_in_psum")
        s_sums_c = sem("row_sums_copied")
        s_root = sem("roots_ready")
        s_d = sem("d_steps")
        s_y1 = sem("y1_supers_ready")
        s_dall = sem("d1_transposed")
        s_drows = sem("d_rows_copied")
        s_dstored = sem("d_row_stored")
        s_dbc = sem("d_broadcast_landed")
        s_lap = sem("lap_ready")
        s_zps = sem("z_in_psum")
        s_prez = sem("pre_z_ready")
        s_z = sem("z_supers_ready")
        s_zsq = sem("z_squares_ready")
        s_sqps = sem("sq_in_psum")
        s_sq = sem("sq_copied")
        s_zh = sem("z_upper_parts_ready")
        s_zl = sem("z_lower_parts_ready")
        s_y2now = sem("y2_now_landed")
        s_y2late = sem("y2_late_landed")
        s_sqt = sem("sq_transposed")
        s_split = sem("sq_split_steps")
        s_sqst = sem("sq_rows_stored")
        s_sqld = sem("sq_rows_landed")
        s_zst = sem("z_blocks_staged")
        s_chunk = sem("score_chunks_in_psum")
        s_evac = sem("score_chunks_copied")
        s_top = sem("tops_ready")
        s_at = sem("tops_located")
        s_kept = sem("tops_kept")
        s_dist = sem("distance_steps")
        s_exp = sem("similarity_steps")
        s_deg = sem("degree_steps")
        s_deg_root = sem("degree_roots_ready")
        s_y2 = sem("y2_supers_ready")
        s_y2st = sem("y2_stored")
        s_xg = sem("x_group_landed")
        s_gath = [sem("gathered_even"), sem("gathered_odd")]
        s_wgt = sem("gathered_weighted")
        s_nsum = sem("near_sums_ready")
        s_turn = sem("near_sums_turned")
        s_tot = sem("totals_ready")
        s_dense = sem("dense_in_psum")
        s_norm = sem("norm_steps")
        s_var = sem("variances_summed")
        s_nroot = sem("norm_roots_ready")
        s_done = sem("rows_done")
        s_xres = [sem("x_res_even"), sem("x_res_odd")]
        s_out = sem("out_stored")

        y2_view = y2_rows.rearrange("(s b p) f -> s p b f", b=PER, p=P)
        b2_row = b2_in.rearrange("(a f) -> a f", a=1)
        block = ctx.enter_context(nc.Block())

        @block.sync
        def _(sp):
            sp.dma_start(y1[:, :], x_in).then_inc(s_x, 16)

            def load_half(tile, ii, gg, h, to, free):
                for s, v in free:
                    sp.wait_ge(s, v)
                if not (isinstance(tile, int) and tile == 0):
                    sp.wait_ge(s_tile[h], tile * 16)
                sp.dma_start(to, adj_in[ds((ii * SUPERS + gg) * 2 + h, 1), :, :].rearrange("a p n -> p (a n)")
                             ).then_inc(s_tile[h], 16)

            def halves_multiplied(u):
                ii, pos = u // (2 * SUPERS), u // 2 % SUPERS
                gg = pos - (SUPERS - 1 - ii)
                return 2 * (tri(ii) + gg) + u % 2 + 1 if gg >= 0 else 2 * tri(ii)

            for n in range(TILES1):
                ii, pos = n // SUPERS, n % SUPERS
                for h in range(2):
                    before = n * 2 + h - SLOTS
                    free = [(s_partial, before + 1)] if before >= 0 else []
                    if before >= 0 and halves_multiplied(before) > 0:
                        free.append((s_prod_half, halves_multiplied(before)))
                    load_half(n, ii, (ii + 1 + pos) % SUPERS, h, ring_slot(n, h), free)

            sp.wait_ge(s_partial, 2 * TILES1)

            def load_high(k, j):
                m = high_product(k, j)[0]
                for h in range(2):
                    v = high_half(k, j, h)
                    if isinstance(v, int) and v < 3:
                        free = [(s_prod_half, v + (2 * LOW - SLOTS + 1))]
                    else:
                        free = [(s_lower, v - 2)]
                    load_half(m + TILE_OF, down(k), high_column(k, j), h, whole_slot(v), free)

            load_high(1, 0)
            load_high(2, 0)
            load_high(2, 1)
            with sp.Fori(3, SUPERS) as k:
                with sp.Fori(0, k) as j:
                    load_high(k, j)

            sp.wait_ge(s_split, 5)
            sp.dma_start(sq_rows.rearrange("r b p -> b r p"), rows_bf[:, :, :]).then_inc(s_sqst, 16)
            sp.wait_ge(s_sqst, 16)
            sp.wait_ge(s_prod_half, 2 * PROD2)
            sq_flat = sq_rows.rearrange("r (q g b) p -> g r q (b p)", g=4, b=BANK // P)
            for g in range(4):
                sp.dma_start(neg_half_sq[32 * g:32 * g + 3, :].rearrange("r (q c) -> r q c", c=BANK),
                             sq_flat[g]).then_inc(s_sqld, 16)

            def behind_searches(gg, ii):
                for h in range(2):
                    m = ii + (gg * SUPERS + PROD2)
                    load_half(m + TILE_OF, ii, gg, h, half_tile[:, :], [(s_prod_half, m * 2 + h)])

            BEHIND = (BLOCKS - LAG) // 2
            for gg in range(EARLY):
                sp.wait_ge(s_y2st, gg * 16 + 16)
                sp.wait_ge(s_prod_half, gg * (2 * SUPERS) + 2 * PROD2)
                sp.dma_start(y2_now[:, :].rearrange("p (b f) -> p b f", f=F),
                             y2_view[gg:gg + 1, :, :, :].rearrange("a p b f -> p (a b) f")).then_inc(s_y2now, 16)
                with sp.Fori(0, min(SUPERS, BEHIND - gg * SUPERS)) as ii:
                    behind_searches(gg, ii)

            def late_half(m, ii, gg, h, slot_no):
                load_half(m + TILE_OF, ii, gg, h, late_ring[:, ds(slot_no * (2 * HCOLS) + h * HCOLS, HCOLS)],
                          [(s_prod_half, m * 2 - 3 + h)])

            sp.wait_ge(s_chunk, BLOCKS * PER)
            with sp.Fori(BEHIND % SUPERS, SUPERS) as ii:
                m = ii + (PROD2 + (EARLY - 1) * SUPERS)
                for h in range(2):
                    late_half(m, ii, EARLY - 1, h, m % 2)

            sp.wait_ge(s_y2st, 16 * SUPERS)
            sp.wait_ge(s_kept, 2 * BLOCKS)
            sp.dma_start(y2_late[:, :].rearrange("p (s b f) -> p s b f", f=F, b=PER),
                         y2_view[EARLY:SUPERS].rearrange("s p b f -> p s b f")).then_inc(s_y2late, 16)

            def late_tile(ii, j):
                for h in range(2):
                    late_half(ii * LATE + j + (PROD2 + EARLY * SUPERS), ii, EARLY + j, h, j % 2)

            def load_x(g, p):
                sp.dma_start(x_res[p], x_in[:, ds(g * SB, SB)]).then_inc(s_xres[p], 16)

            def store(g):
                sp.wait_ge(s_done, g + 1)
                sp.dma_start(out[:, ds(g * SB, SB)], row_out[:, :]).then_inc(s_out, 16)

            load_x(0, 0)
            load_x(1, 1)
            with sp.Fori(0, 2) as ii:
                for j in range(LATE):
                    late_tile(ii, j)
            with sp.Fori(1, SUPERS // 2) as q:
                for p in range(2):
                    for j in range(LATE):
                        late_tile(q * 2 + p, j)
                        if j == 0:
                            store(q * 2 + p - 2)
                            load_x(q * 2 + p, p)
            store(SUPERS - 2)
            store(SUPERS - 1)
            sp.wait_ge(s_out, 16 * SUPERS)

        @block.gpsimd
        def _(pool):
            pool.dma_start(w1[:, :], w1_in).then_inc(s_const, 16)
            pool.dma_start(w2[:, :], w2_in).then_inc(s_const, 16)
            pool.dma_start(b1[:, :], b1_in.rearrange("(f a) -> f a", a=1)).then_inc(s_const, 16)
            pool.dma_start(b2[:, :], b2_row.to_broadcast([P, F])).then_inc(s_const, 16)
            nc.gpsimd.memset(ident[:, :], 0.0).then_inc(s_memset, 1)
            pool.wait_ge(s_memset, 1)
            nc.gpsimd.affine_select(out=ident[:, :], in_=ident[:, :], compare_op=ALU.not_equal, fill=1.0, base=0,
                                    pattern=[[-1, P]], channel_multiplier=1).then_inc(s_memset, 1)
            nc.gpsimd.memset(ones[:, :], 1.0).then_inc(s_memset, 1)
            nc.gpsimd.memset(ones_bf[:, :], 1.0).then_inc(s_memset, 1)
            nc.gpsimd.memset(conv1_t[:, :], 0.0).then_inc(s_zeroed, 1)

            def add_partial(count, h):
                pool.wait_ge(s_partial, count + 1)
                pool.wait_ge(s_acc, count)
                nc.gpsimd.tensor_tensor(acc[:, :], acc[:, :], partial[h][:, :], ALU.add).then_inc(s_acc, 1)

            with pool.Fori(0, SUPERS) as ii:
                pool.wait_ge(s_sums, ii)
                pool.wait_ge(s_partial, ii * (2 * SUPERS) + 2)
                nc.gpsimd.tensor_tensor(acc[:, :], partial[0][:, :], partial[1][:, :], ALU.add).then_inc(s_acc, 2)
                with pool.Fori(1, SUPERS) as k:
                    for h in range(2):
                        add_partial((ii * SUPERS + k) * 2 + h, h)

            pool.wait_ge(s_drows, 1)
            pool.dma_start(d_row, rows_t[:, 0, :]).then_inc(s_dstored, 16)
            pool.wait_ge(s_dstored, 16)
            d_flat = d_row.rearrange("(s b) p -> s (b p)", b=PER)

            def load_d(k):
                if not (isinstance(k, int) and k == 0):
                    pool.wait_ge(s_lap, k)
                pool.dma_start(d_bcast[:, :], d_flat[ds(down(k), 1), :].to_broadcast([P, SB])).then_inc(s_dbc, 16)

            def lower_y(k, j):
                for h in range(2):
                    pool.wait_ge(s_staged, high_half(k, j, h) + (2 * LOW + 1))
                    nc.gpsimd.tensor_tensor(
                        y_stage_l[:, h, :], y1[:, ds(high_column(k, j) * (PER * F) + h * (HALF * F), HALF * F)],
                        y_stage_h[:, h, :].bitcast(fp32), ALU.subtract).then_inc(s_ylow, 1)

            load_d(0)
            lower_y(1, 0)
            load_d(1)
            for j in range(2):
                lower_y(2, j)
            load_d(2)
            with pool.Fori(3, SUPERS) as k:
                for j in range(2):
                    lower_y(k, j)
                load_d(k)
                with pool.Fori(2, k) as j:
                    lower_y(k, j)

            pool.wait_ge(s_prod_half, 2 * PROD2)
            nc.gpsimd.memset(conv2_t[:, :], 0.0).then_inc(s_zeroed, 1)

            def load_group(g):
                pool.dma_start(x_y2[:, :], x_in[:, ds(g * SB, SB)]).then_inc(s_xg, 16)

            def store_group(g):
                pool.wait_ge(s_y2, g + 1)
                pool.dma_start(y2_view[ds(g, 1), :, :, :].rearrange("a p b f -> p (a b) f"),
                               x_y2[:, :].rearrange("p (b f) -> p b f", f=F)).then_inc(s_y2st, 16)

            load_group(0)
            with pool.Fori(0, SUPERS - 1) as g:
                store_group(g)
                pool.wait_ge(s_y2st, g * 16 + 16)
                load_group(g + 1)
            store_group(SUPERS - 1)

            pool.wait_ge(s_kept, 2 * BLOCKS)
            pool.wait_ge(s_y2st, 16 * SUPERS)
            for g in range(SUPERS):
                if g >= 2:
                    pool.wait_ge(s_nsum, g - 1)
                for j in range(PER * K):
                    nc.gpsimd.indirect_dma_start(
                        gathered[g % 2][:, j * F:(j + 1) * F], None, y2_rows,
                        bass.IndirectOffsetOnAxis(ap=near[:, g * PER + j // K, j % K:j % K + 1], axis=0)
                    ).then_inc(s_gath[g % 2], 16)

        @block.scalar
        def _(act):
            def stage_y(product, gg, ready):
                act.wait_ge(s_y1, ready)
                for h in range(2):
                    if not (isinstance(product[0], int) and product[0] == 0):
                        act.wait_ge(s_prod_half, product[2] - 1 + h)
                    nc.scalar.copy(y_stage[:, h, :], y1[:, ds(gg * (PER * F) + h * (HALF * F), HALF * F)]
                                   ).then_inc(s_staged, 1)

            def root(ii):
                act.wait_ge(s_sums_c, ii + 1)
                nc.scalar.activation(small[:, 1, :], small[:, 0, :], ACT.Sqrt).then_inc(s_root, 1)

            root(0)
            stage_y(low_product(0, 0), 0, 1)
            with act.Fori(1, SUPERS) as ii:
                with act.Fori(0, ii) as gg:
                    stage_y(low_product(ii, gg), gg, 1)
                root(ii)
                stage_y(low_product(ii, ii), ii, ii + 1)

            def pre_activation(k):
                act.wait_ge(s_zps, k + 1)
                nc.scalar.activation(pre_z[:, :], z_ps, ACT.Identity, bias=b1[:, 0:1]).then_inc(s_prez, 1)

            def square(k):
                act.wait_ge(s_z, k + 1)
                nc.scalar.activation(z_sq[:, :], conv1_t[:, ds(down(k) * SB, SB)], ACT.Square).then_inc(s_zsq, 1)

            def upper_y(k, j, h):
                act.wait_ge(s_prod_half, high_half(k, j, h) + (2 * LOW - 1))
                nc.scalar.copy(y_stage_h[:, h, :], y1[:, ds(high_column(k, j) * (PER * F) + h * (HALF * F), HALF * F)]
                               ).then_inc(s_staged, 1)

            def upper_tile_half(k, j, h):
                v = high_half(k, j, h)
                if isinstance(v, int) and v < 2:
                    act.wait_ge(s_prod_half, v + (2 * LOW - 3))
                else:
                    act.wait_ge(s_upper_used, v - 1)
                    act.wait_ge(s_lower, v - 1)
                act.wait_ge(s_tile[h], high_product(k, j)[0] * 16 + (TILE_OF * 16 + 16))
                nc.scalar.copy(upper_slot(v), whole_slot(v)).then_inc(s_upper, 1)

            def upper_parts(k, j, after):
                upper_y(k, j, 0)
                upper_tile_half(k, j, 1)
                upper_y(k, j, 1)
                if after is not None:
                    upper_tile_half(after[0], after[1], 0)

            upper_tile_half(1, 0, 0)
            upper_parts(1, 0, (2, 0))
            pre_activation(0)
            upper_parts(2, 0, (2, 1))
            square(0)
            pre_activation(1)
            upper_parts(2, 1, (3, 0))
            square(1)
            with act.Fori(3, SUPERS - 1) as k:
                upper_parts(k, 0, (k, 1))
                pre_activation(k - 1)
                with act.Fori(1, k - 1) as j:
                    upper_parts(k, j, (k, j + 1))
                upper_parts(k, k - 1, (k + 1, 0))
                square(k - 1)
            last = SUPERS - 1
            upper_parts(last, 0, (last, 1))
            pre_activation(last - 1)
            with act.Fori(1, last - 1) as j:
                upper_parts(last, j, (last, j + 1))
            upper_parts(last, last - 1, None)
            square(last - 1)
            pre_activation(last)
            square(last)
            act.wait_ge(s_sqps, SUPERS)
            for c in range(SUPERS):
                nc.scalar.copy(z_h[:, c * SB:(c + 1) * SB], conv1_t[:, c * SB:(c + 1) * SB]).then_inc(s_zh, 1)

            def search(t, p, first=False):
                if not first:
                    act.wait_ge(s_chunk, t * PER - PER)
                nc.scalar.copy(z_stage_h[:, p, :], z_h[:, ds(t * P, P)].bitcast(fp32))
                nc.scalar.copy(z_stage_l[:, p, :], z_l[:, ds(t * P, P)].bitcast(fp32)).then_inc(s_zst, 1)
                if not first:
                    act.wait_ge(s_at, t - 1)
                for c in range(PER):
                    act.wait_ge(s_chunk, t * PER + c + 1)
                    nc.scalar.copy(scores[p][:, c * SB:(c + 1) * SB],
                                   score_ps[:, (c % 2) * SB:(c % 2 + 1) * SB]).then_inc(s_evac, 1)

            def similarities(g):
                act.wait_ge(s_dist, g * 2 + 2)
                nc.scalar.activation(dist[:, 0], dist[:, 0], ACT.Sqrt).then_inc(s_exp, 1)
                act.wait_ge(s_exp, g * 2 + 1)
                nc.scalar.activation(dist[:, 1], dist[:, 0], ACT.Exp, scale=-0.5).then_inc(s_exp, 1)
                act.wait_ge(s_deg, g * 4 + 2)
                nc.scalar.activation(small[:, 1, :], small[:, 0, :], ACT.Sqrt).then_inc(s_deg_root, 1)

            def segment(g):
                with act.Fori(0, PER // 2 - 1) as q:
                    for p in range(2):
                        search(g * PER + q * 2 + 2 + p, p)
                for p in range(2):
                    search(g * PER + PER + p, p)
                similarities(g)

            act.wait_ge(s_zl, SUPERS)
            act.wait_ge(s_prod_half, 2 * PROD2)
            search(0, 0, True)
            search(1, 1, True)
            with act.Fori(0, SUPERS - 1) as g:
                segment(g)
            with act.Fori(0, PER // 2 - 1) as q:
                for p in range(2):
                    search(q * 2 + BLOCKS - PER + 2 + p, p)
            similarities(SUPERS - 1)

            with act.Fori(0, SUPERS) as g:
                act.wait_ge(s_norm, g * 8 + 7)
                nc.scalar.activation(stat[:, 2, :], stat[:, 1, :], ACT.Sqrt).then_inc(s_nroot, 1)

        @block.vector
        def _(dve):
            def sum_tile(n):
                for h in range(2):
                    dve.wait_ge(s_tile[h], n * 16 + 16)
                    if not (isinstance(n, int) and n == 0):
                        dve.wait_ge(s_acc, n * 2 - 1 + h)
                    nc.vector.tensor_reduce(
                        partial[h][:, :],
                        ring_slot(n, h).rearrange("p (b i) -> p i b", b=HALF),
                        X, ALU.add).then_inc(s_partial, 1)

            def add_product(product, target, at):
                m, _, halves = product
                dve.wait_ge(s_prod_half, halves + 2)
                dve.wait_ge(s_added, m)
                nc.vector.tensor_tensor(target[:, ds(at, SB)], target[:, ds(at, SB)],
                                        prod_ps[:, ds((m % 2) * SB, SB)], ALU.add).then_inc(s_added, 1)

            def finish_rows(ii):
                dve.wait_ge(s_sums, ii + 1)
                nc.vector.tensor_copy(small[:, 0, :], sums_ps).then_inc(s_sums_c, 1)
                nc.vector.tensor_copy(row_sum[:, ds(ii * PER, PER)], sums_ps)
                dve.wait_ge(s_root, ii + 1)
                nc.vector.reciprocal(small[:, 2, :], small[:, 1, :]).then_inc(s_d, 1)
                dve.wait_ge(s_d, ii * 2 + 1)
                nc.vector.tensor_copy(d1[:, ds(ii * PER, PER)], small[:, 2, :]).then_inc(s_d, 1)
                v = y1[:, ds(ii * SB, SB)].rearrange("p (b f) -> p b f", f=F)
                nc.vector.tensor_tensor(v, v, small[:, 2, :].unsqueeze(2).to_broadcast([P, PER, F]),
                                        ALU.mult).then_inc(s_y1, 1)

            dve.wait_ge(s_x, 16)
            for n in range(SUPERS):
                sum_tile(n)
            finish_rows(0)
            dve.wait_ge(s_zeroed, 1)

            def sum_row(ii, upper, longer):
                if upper:
                    with dve.Fori(ii + 1, SUPERS) as gg:
                        sum_tile(upper_tile(ii, gg))
                add_product(low_product(ii - 1, ii - 1), conv1_t, ii * SB - SB)
                sum_tile(lower_tile(ii, 0))
                if longer:
                    with dve.Fori(1, ii) as gg:
                        sum_tile(lower_tile(ii, gg))
                        add_product(low_product(ii, gg - 1), conv1_t, ii * SB)
                sum_tile(lower_tile(ii, ii))
                finish_rows(ii)
                add_product(low_product(ii, ii - 1), conv1_t, ii * SB)

            sum_row(1, True, False)
            with dve.Fori(2, SUPERS - 1) as ii:
                sum_row(ii, True, True)
            last = SUPERS - 1
            sum_row(last, False, True)
            dve.wait_ge(s_dall, 1)
            nc.vector.tensor_copy(rows_t[:, 0, :], rows_ps).then_inc(s_drows, 1)
            add_product(numbered(LOW - 1), conv1_t, last * SB)

            def lap(k, added):
                dve.wait_ge(s_dbc, k * 16 + 16)
                dve.wait_ge(s_added, added)
                if not (isinstance(k, int) and k == 0):
                    dve.wait_ge(s_zps, k)
                nc.vector.tensor_tensor(lap_t[:, :], conv1_t[:, ds(down(k) * SB, SB)], d_bcast[:, :],
                                        ALU.mult).then_inc(s_lap, 1)

            def leaky(k):
                dve.wait_ge(s_prez, k + 1)
                nc.vector.scalar_tensor_tensor(conv1_t[:, ds(down(k) * SB, SB)], pre_z[:, :], 0.1, pre_z[:, :],
                                               ALU.mult, ALU.max).then_inc(s_z, 1)

            def copy_sq(k):
                dve.wait_ge(s_sqps, k + 1)
                nc.vector.tensor_copy(sq[:, ds(down(k) * PER, PER)], sums_ps).then_inc(s_sq, 1)

            def lower_tile_parts(k, j):
                for h in range(2):
                    v = high_half(k, j, h)
                    dve.wait_ge(s_upper, v + 1)
                    dve.wait_ge(s_prod_half, v + (2 * LOW - 1))
                    nc.vector.tensor_tensor(lower_slot(v), whole_slot(v), upper_slot(v).bitcast(fp32),
                                            ALU.subtract).then_inc(s_lower, 1)

            lap(0, LOW)
            lower_tile_parts(1, 0)
            leaky(0)
            lower_tile_parts(2, 0)
            add_product(high_product(1, 0), conv1_t, down(1) * SB)
            lap(1, high_product(2, 0)[0])
            lower_tile_parts(2, 1)
            add_product(high_product(2, 0), conv1_t, down(2) * SB)
            leaky(1)
            copy_sq(0)
            with dve.Fori(3, SUPERS) as k:
                lower_tile_parts(k, 0)
                add_product(high_product(k - 1, k - 2), conv1_t, down(k - 1) * SB)
                copy_sq(k - 2)
                lap(k - 1, high_product(k, 0)[0])
                lower_tile_parts(k, 1)
                add_product(high_product(k, 0), conv1_t, down(k) * SB)
                leaky(k - 1)
                with dve.Fori(2, k) as j:
                    lower_tile_parts(k, j)
                    add_product(high_product(k, j - 1), conv1_t, down(k) * SB)
            add_product(high_product(last, last - 1), conv1_t, 0)
            copy_sq(last - 1)
            lap(last, PROD2)
            leaky(last)
            copy_sq(last)

            dve.wait_ge(s_sqt, 1)
            nc.vector.tensor_scalar(rows_t[:, 1, :], rows_ps, -0.5, None, ALU.mult).then_inc(s_split, 1)
            dve.wait_ge(s_split, 1)
            nc.vector.tensor_copy(rows_bf[:, 0, :], rows_t[:, 1, :]).then_inc(s_split, 1)
            dve.wait_ge(s_split, 2)
            nc.vector.tensor_tensor(rows_t[:, 2, :], rows_t[:, 1, :], rows_bf[:, 0, :],
                                    ALU.subtract).then_inc(s_split, 1)
            dve.wait_ge(s_split, 3)
            nc.vector.tensor_copy(rows_bf[:, 1, :], rows_t[:, 2, :]).then_inc(s_split, 1)
            dve.wait_ge(s_split, 4)
            nc.vector.tensor_tensor(rows_bf[:, 2, :], rows_t[:, 2, :], rows_bf[:, 1, :],
                                    ALU.subtract).then_inc(s_split, 1)

            for c in range(SUPERS):
                dve.wait_ge(s_zh, c + 1)
                nc.vector.tensor_tensor(z_l[:, c * SB:(c + 1) * SB], conv1_t[:, c * SB:(c + 1) * SB],
                                        z_h[:, c * SB:(c + 1) * SB].bitcast(fp32), ALU.subtract).then_inc(s_zl, 1)

            def search(t, p):
                dve.wait_ge(s_evac, t * PER + PER)
                nc.vector.tensor_copy(gate[:, 0:1], ones[:, :])
                nc.vector.max(top[:, p, :], scores[p][:, :]).then_inc(s_top, 1)
                dve.wait_ge(s_top, t + 1)
                nc.vector.tensor_copy(best[:, ds(t, 1), :].rearrange("p a k -> p (a k)"),
                                      top[:, p, 0:K]).then_inc(s_kept, 1)
                nc.vector.max_index(top_at[:, p, :], top[:, p, :], scores[p][:, :]).then_inc(s_at, 1)
                dve.wait_ge(s_at, t + 1)
                nc.vector.tensor_copy(near[:, ds(t, 1), :].rearrange("p a k -> p (a k)"),
                                      top_at[:, p, 0:K]).then_inc(s_kept, 1)

            def follow(pair):
                u = pair - LAG // 2
                add_product(numbered(u + PROD2), conv2_t, (u % SUPERS) * SB)

            def new_degrees(g, kept):
                at = ds(g * PER, PER)
                dve.wait_ge(s_kept, kept)
                nc.vector.scalar_tensor_tensor(dist[:, 0], best[:, at, :], -2.0,
                                               sq[:, at].unsqueeze(2).to_broadcast([P, PER, K]),
                                               ALU.mult, ALU.add).then_inc(s_dist, 1)
                dve.wait_ge(s_dist, g * 2 + 1)
                nc.vector.tensor_scalar(dist[:, 0], dist[:, 0], 0.0, EPS_DIST, ALU.max, ALU.add).then_inc(s_dist, 1)
                dve.wait_ge(s_exp, g * 2 + 2)
                nc.vector.tensor_reduce(small[:, 3, :], dist[:, 1], X, ALU.add).then_inc(s_deg, 1)
                nc.vector.tensor_copy(sim[:, at, :], dist[:, 1])
                dve.wait_ge(s_deg, g * 4 + 1)
                nc.vector.tensor_tensor(small[:, 0, :], small[:, 3, :], row_sum[:, at], ALU.add).then_inc(s_deg, 1)
                dve.wait_ge(s_deg_root, g + 1)
                nc.vector.reciprocal(small[:, 2, :], small[:, 1, :]).then_inc(s_deg, 1)
                dve.wait_ge(s_deg, g * 4 + 3)
                nc.vector.tensor_copy(d2[:, at], small[:, 2, :]).then_inc(s_deg, 1)
                dve.wait_ge(s_xg, g * 16 + 16)
                v = x_y2[:, :].rearrange("p (b f) -> p b f", f=F)
                nc.vector.tensor_tensor(v, v, small[:, 2, :].unsqueeze(2).to_broadcast([P, PER, F]),
                                        ALU.mult).then_inc(s_y2, 1)

            def segment(g, with_products):
                with dve.Fori(0, PER // 2 - 1) as q:
                    for p in range(2):
                        search(g * PER + q * 2 + 2 + p, p)
                    if with_products:
                        follow(g * (PER // 2) + q + 1)
                search(g * PER + PER, 0)
                new_degrees(g, (g * PER + PER + 1) * 2)
                search(g * PER + PER + 1, 1)
                if with_products:
                    follow(g * (PER // 2) + PER // 2)

            search(0, 0)
            search(1, 1)
            segment(0, False)
            dve.wait_ge(s_zeroed, 2)
            with dve.Fori(1, SUPERS - 1) as g:
                segment(g, True)
            with dve.Fori((BLOCKS - PER) // 2 + 1, BLOCKS // 2) as pair:
                search(pair * 2, 0)
                search(pair * 2 + 1, 1)
                follow(pair)
            new_degrees(SUPERS - 1, 2 * BLOCKS)
            with dve.Fori(BLOCKS // 2, (BLOCKS + LAG) // 2) as pair:
                follow(pair)

            def late_sums(g, q, p):
                rows = gathered[p][:, :].rearrange("p (b k f) -> p b k f", k=K, f=F)
                dve.wait_ge(s_gath[p], (q + 1) * (16 * PER * K))
                for b in range(PER):
                    w = nc.vector.tensor_tensor(
                        rows[:, b], rows[:, b],
                        sim[:, ds(g * PER + b, 1), :].rearrange("p a k -> p (a k)").unsqueeze(2).to_broadcast([P, K, F]),
                        ALU.mult)
                w.then_inc(s_wgt, 1)
                dve.wait_ge(s_wgt, g + 1)
                if not (isinstance(g, int) and g == 0):
                    dve.wait_ge(s_turn, g)
                nc.vector.tensor_reduce(near_sum[:, :].rearrange("p (b f) -> p b f", f=F),
                                        rows.rearrange("p b k f -> p b f k"), X, ALU.add).then_inc(s_nsum, 1)

            def totals(g):
                dve.wait_ge(s_prod_half, g * (2 * LATE) + 2 * (PROD2 + EARLY * SUPERS + LATE))
                nc.vector.tensor_tensor(conv2_t[:, ds(g * SB, SB)], conv2_t[:, ds(g * SB, SB)],
                                        prod_ps[:, ds((g % 2) * SB, SB)], ALU.add).then_inc(s_added, 1)
                dve.wait_ge(s_added, g + (PROD2 + EARLY * SUPERS + 1))
                dve.wait_ge(s_turn, g + 1)
                if not (isinstance(g, int) and g == 0):
                    dve.wait_ge(s_dense, g)
                nc.vector.tensor_tensor(total_t[:, :], turned_ps, conv2_t[:, ds(g * SB, SB)],
                                        ALU.add).then_inc(s_tot, 1)

            def finish(g, q, p):
                at = ds(g * PER, PER)
                out3 = row_out[:, :].rearrange("p (b f) -> p b f", f=F)
                sq3 = row_sq[:, :].rearrange("p (b f) -> p b f", f=F)
                dve.wait_ge(s_dense, g + 1)
                if not (isinstance(g, int) and g == 0):
                    dve.wait_ge(s_out, g * 16)
                n = [0]

                def step(ins):
                    n[0] += 1
                    ins.then_inc(s_norm, 1)
                    dve.wait_ge(s_norm, g * 8 + n[0])

                step(nc.vector.tensor_tensor(out3, dense_ps.rearrange("p (b f) -> p b f", f=F),
                                             d2[:, at].unsqueeze(2).to_broadcast([P, PER, F]), ALU.mult))
                step(nc.vector.tensor_tensor(out3, out3, b2[:, :].unsqueeze(1).to_broadcast([P, PER, F]), ALU.add))
                dve.wait_ge(s_xres[p], q * 16 + 16)
                step(nc.vector.tensor_tensor(row_out[:, :], row_out[:, :], x_res[p][:, :], ALU.add))
                step(nc.vector.tensor_reduce(stat[:, 0, :], out3, X, ALU.add))
                nc.vector.scalar_tensor_tensor(out3, stat[:, 0, :].unsqueeze(2).to_broadcast([P, PER, F]), -1.0 / F,
                                               out3, ALU.mult, ALU.add).then_inc(s_norm, 1)
                dve.wait_ge(s_norm, g * 8 + 5)
                nc.vector.tensor_tensor(row_sq[:, :], row_out[:, :], row_out[:, :], ALU.mult).then_inc(s_norm, 1)
                dve.wait_ge(s_norm, g * 8 + 6)
                nc.vector.tensor_reduce(stat[:, 0, :], sq3, X, ALU.add).then_inc(s_var, 1)
                dve.wait_ge(s_var, g + 1)
                nc.vector.tensor_scalar(stat[:, 1, :], stat[:, 0, :], 1.0 / F, EPS_NORM, ALU.mult,
                                        ALU.add).then_inc(s_norm, 1)
                dve.wait_ge(s_nroot, g + 1)
                nc.vector.reciprocal(stat[:, 3, :], stat[:, 2, :]).then_inc(s_norm, 1)
                dve.wait_ge(s_norm, g * 8 + 8)
                nc.vector.tensor_tensor(out3, out3, stat[:, 3, :].unsqueeze(2).to_broadcast([P, PER, F]),
                                        ALU.mult).then_inc(s_done, 1)


            dve.wait_ge(s_added, PROD2 + EARLY * SUPERS)
            late_sums(0, 0, 0)
            totals(0)
            late_sums(1, 0, 1)
            finish(0, 0, 0)
            totals(1)
            with dve.Fori(1, SUPERS // 2) as q:
                late_sums(q * 2, q, 0)
                finish(q * 2 - 1, q - 1, 1)
                totals(q * 2)
                late_sums(q * 2 + 1, q, 1)
                finish(q * 2, q, 0)
                totals(q * 2 + 1)
            finish(SUPERS - 1, SUPERS // 2 - 1, 1)

        @block.tensor
        def _(pe):
            def half_product(m, tile, h, stationary, moving, start, stop):
                pe.wait_ge(s_tile[h], tile * 16 + 16)
                for b in range(HALF):
                    for c in range(SB // BANK):
                        last = nc.tensor.matmul(
                            prod_ps[:, ds((m % 2) * SB + c * BANK, BANK)], stationary(b),
                            moving(b * SB + c * BANK), start=start and b == 0, stop=stop and b == HALF - 1)
                last.then_inc(s_prod_half, 1)

            def product(number, tile, between=None):
                m, before, halves = number
                if not (isinstance(m, int) and m < 2):
                    pe.wait_ge(s_added, before)
                for h in range(2):
                    pe.wait_ge(s_staged, halves + h + 1)
                    half_product(m, tile, h, lambda b: y_stage[:, h, b * F:(b + 1) * F],
                                 lambda at: ring_slot(tile, h, at, BANK),
                                 h == 0, h == 1)
                    if h == 0 and between is not None:
                        between()

            def row_sums(ii):
                pe.wait_ge(s_acc, ii * (2 * SUPERS) + 2 * SUPERS)
                if not (isinstance(ii, int) and ii == 0):
                    pe.wait_ge(s_d, ii * 2)
                for b in range(PER):
                    last = nc.tensor.matmul(sums_ps[:, b:b + 1], acc[:, b * P:(b + 1) * P], ones[:, :],
                                            start=True, stop=True)
                last.then_inc(s_sums, 1)

            pe.wait_ge(s_memset, 4)
            pe.wait_ge(s_const, 64)
            def row(ii, longer, within):
                if longer:
                    with pe.Fori(0, ii - 1) as gg:
                        product(low_product(ii, gg), lower_tile(ii, gg))
                product(low_product(ii, ii - 1), lower_tile(ii, ii - 1), (lambda: row_sums(ii)) if within else None)
                if not within:
                    row_sums(ii)
                product(low_product(ii, ii), lower_tile(ii, ii))

            row_sums(0)
            product(low_product(0, 0), lower_tile(0, 0))
            row(1, False, False)
            with pe.Fori(2, SUPERS - 2) as ii:
                row(ii, True, False)
            with pe.Fori(SUPERS - 2, SUPERS) as ii:
                row(ii, True, True)
            pe.wait_ge(s_d, 2 * SUPERS)
            nc.tensor.matmul(rows_ps, d1[:, :], ident[:, :], start=True, stop=True).then_inc(s_dall, 1)

            def first_layer(k):
                pe.wait_ge(s_lap, k + 1)
                if not (isinstance(k, int) and k == 0):
                    pe.wait_ge(s_prez, k)
                else:
                    pe.wait_ge(s_drows, 1)
                for c in range(SB // BANK):
                    last = nc.tensor.matmul(z_ps[:, c * BANK:(c + 1) * BANK], w1[:, :],
                                            lap_t[:, c * BANK:(c + 1) * BANK], start=True, stop=True)
                last.then_inc(s_zps, 1)

            def squares(k):
                pe.wait_ge(s_zsq, k + 1)
                if not (isinstance(k, int) and k == 0):
                    pe.wait_ge(s_sq, k)
                for b in range(PER):
                    last = nc.tensor.matmul(sums_ps[:, b:b + 1], z_sq[:, b * P:(b + 1) * P], ones[:, :],
                                            start=True, stop=True)
                last.then_inc(s_sqps, 1)

            def high(k, j):
                m, before, _ = high_product(k, j)
                pe.wait_ge(s_added, before)
                for h in range(2):
                    v = high_half(k, j, h)
                    passes = ((y_stage_h, upper_slot, s_staged, 2 * LOW), (y_stage_l, upper_slot, s_ylow, 0),
                              (y_stage_h, lower_slot, s_lower, 0))
                    for i, (still, moving, ready, earlier) in enumerate(passes):
                        if i == 0:
                            pe.wait_ge(s_upper, v + 1)
                        pe.wait_ge(ready, v + (earlier + 1))
                        for b in range(HALF):
                            for c in range(SB // BANK):
                                last = nc.tensor.matmul(
                                    prod_ps[:, ds((m % 2) * SB + c * BANK, BANK)], still[:, h, b * F:(b + 1) * F],
                                    moving(v, b * SB + c * BANK, BANK),
                                    start=h == 0 and i == 0 and b == 0, stop=h == 1 and i == 2 and b == HALF - 1)
                        if i == 1:
                            last.then_inc(s_upper_used, 1)
                    last.then_inc(s_prod_half, 1)

            high(1, 0)
            first_layer(0)
            high(2, 0)
            squares(0)
            first_layer(1)
            high(2, 1)
            squares(1)
            with pe.Fori(3, SUPERS) as k:
                high(k, 0)
                first_layer(k - 1)
                with pe.Fori(1, k) as j:
                    high(k, j)
                squares(k - 1)
            first_layer(SUPERS - 1)
            squares(SUPERS - 1)
            pe.wait_ge(s_sq, SUPERS)
            nc.tensor.matmul(rows_ps, sq[:, :], ident[:, :], start=True, stop=True).then_inc(s_sqt, 1)

            def search(t, p, first=False):
                pe.wait_ge(s_zst, t + 1)
                for c in range(PER):
                    if not (first and c < 2):
                        pe.wait_ge(s_evac, t * PER + c - 1)
                    for half in range(SB // BANK):
                        n = c * (SB // BANK) + half
                        grp = 32 * (n % 4)
                        nc.tensor.matmul(score_ps[:, (c % 2) * SB + half * BANK:(c % 2) * SB + (half + 1) * BANK],
                                         ones_bf[grp:grp + 3, :],
                                         neg_half_sq[grp:grp + 3, (n // 4) * BANK:(n // 4 + 1) * BANK],
                                         start=True, stop=False)
                    for i, (still, moving) in enumerate(((z_stage_h, z_h), (z_stage_h, z_l), (z_stage_l, z_h))):
                        for half in range(SB // BANK):
                            n = c * (SB // BANK) + half
                            last = nc.tensor.matmul(
                                score_ps[:, (c % 2) * SB + half * BANK:(c % 2) * SB + (half + 1) * BANK],
                                still[:, p, :], moving[:, n * BANK:(n + 1) * BANK], start=False, stop=(i == 2))
                    last.then_inc(s_chunk, 1)

            def follow(pair, h, tile=lambda m, at: half_tile[:, at:at + BANK]):
                u = pair - LAG // 2
                m = u + PROD2
                if h == 0:
                    pe.wait_ge(s_added, m - 1)
                    pe.wait_ge(s_y2now, (u // SUPERS) * 16 + 16)
                half_product(m, m + TILE_OF, h, lambda b: y2_now[:, (h * HALF + b) * F:(h * HALF + b + 1) * F],
                             lambda at: tile(m, at), h == 0, h == 1)

            pe.wait_ge(s_split, 1)
            pe.wait_ge(s_sqld, 64)
            search(0, 0, True)
            search(1, 1)
            with pe.Fori(1, PER // 2 + 1) as q:
                for p in range(2):
                    search(q * 2 + p, p)
            with pe.Fori(LAG // 2, BLOCKS // 2) as q:
                for p in range(2):
                    search(q * 2 + p, p)
                    follow(q, p)
            with pe.Fori(BLOCKS // 2, (BLOCKS + LAG) // 2) as q:
                for p in range(2):
                    follow(q, p, lambda m, at: late_ring[:, ds((m % 2) * (2 * HCOLS) + p * HCOLS + at, BANK)])

            def turn(g):
                pe.wait_ge(s_nsum, g + 1)
                if not (isinstance(g, int) and g == 0):
                    pe.wait_ge(s_tot, g)
                for b in range(PER):
                    last = nc.tensor.matmul(turned_ps[:, b * P:(b + 1) * P], near_sum[:, b * F:(b + 1) * F],
                                            ident[:, :], start=True, stop=True)
                last.then_inc(s_turn, 1)

            def dense(g):
                pe.wait_ge(s_tot, g + 1)
                if not (isinstance(g, int) and g == 0):
                    pe.wait_ge(s_norm, g * 8 - 7)
                for b in range(PER):
                    last = nc.tensor.matmul(dense_ps[:, b * F:(b + 1) * F], total_t[:, b * P:(b + 1) * P],
                                            w2[:, :], start=True, stop=True)
                last.then_inc(s_dense, 1)

            def late_products(ii, after_first):
                pe.wait_ge(s_added, ii + (PROD2 + EARLY * SUPERS - 1))
                for j in range(LATE):
                    m = ii * LATE + j + (PROD2 + EARLY * SUPERS)
                    for h in range(2):
                        half_product(ii, m + TILE_OF, h,
                                     lambda b: y2_late[:, j * SB + (h * HALF + b) * F:j * SB + (h * HALF + b + 1) * F],
                                     lambda at: late_ring[:, (j % 2 * 2 + h) * HCOLS + at:(j % 2 * 2 + h) * HCOLS + at + BANK],
                                     j == 0 and h == 0, j == LATE - 1 and h == 1)
                    if j == 0 and after_first:
                        dense(ii - 1)
                turn(ii)

            pe.wait_ge(s_y2late, 16)
            late_products(0, False)
            late_products(1, True)
            with pe.Fori(2, SUPERS) as ii:
                late_products(ii, True)
            dense(SUPERS - 1)


def kernel(x, adj, L0_gnn_W1, L0_gnn_b1, L0_gnn_W2, L0_gnn_b2):
    import numpy as np
    import concourse.bacc as bacc
    from concourse import mybir as _mybir
    from concourse.bass_utils import run_bass_kernel_spmd as run

    x, adj = np.asarray(x), np.asarray(adj)
    n, f = x.shape
    p, sb = 128, 1024
    supers, half = n // sb, sb // p // 2
    x_part = np.ascontiguousarray(x.reshape(n // p, p, f).transpose(1, 0, 2)).reshape(p, n // p * f)
    tiles = np.ascontiguousarray(adj.reshape(supers, sb, supers, 2, half, p).transpose(0, 2, 3, 5, 4, 1))
    tiles = tiles.reshape(supers * supers * 2, p, half * sb)
    arrays = {"x_part": x_part, "adj_tiles": tiles, "w1_dram": np.ascontiguousarray(L0_gnn_W1),
              "b1_dram": np.ascontiguousarray(L0_gnn_b1), "w2_dram": np.ascontiguousarray(L0_gnn_W2),
              "b2_dram": np.ascontiguousarray(L0_gnn_b2)}
    nc = bacc.Bacc("TRN2", target_bir_lowering=False, num_devices=1)
    args = [nc.dram_tensor(k, a.shape, _mybir.dt.from_np(a.dtype), kind="ExternalInput").ap()
            for k, a in arrays.items()]
    out = nc.dram_tensor("out", (p, n // p * f), _mybir.dt.float32, kind="ExternalOutput").ap()
    resnorm_graph_kernel(nc, *args, out)
    r = run(nc, [arrays], core_ids=[0])
    got = np.asarray(r.results[0]["out"])
    return np.ascontiguousarray(got.reshape(p, n // p, f).transpose(1, 0, 2)).reshape(n, f)
```

```python
import concourse.bass as bass
from concourse import mybir
from contextlib import ExitStack



def resnorm_graph_kernel(nc, x_in, adj_in, w1_in, b1_in, w2_in, b2_in, out):
    fp32 = mybir.dt.float32
    bf16 = mybir.dt.bfloat16
    u32 = mybir.dt.uint32
    fp32r = mybir.dt.float32r
    ALU = mybir.AluOpType
    ACT = mybir.ActivationFunctionType
    X = mybir.AxisListType.X
    ds = bass.ds

    P = 128

    N = P * (x_in.shape[1] // P)
    BLOCKS = N // P
    SB = adj_in.shape[2] // 4
    SUPERS = N // SB
    PER = SB // P
    HALF = PER // 2
    HCOLS = HALF * SB
    BANK = 512
    K = 4
    EPS_DIST, EPS_NORM = 1e-10, 1e-5
    F = P
    LATE_ROW = SUPERS - 2
    SPLIT_FIRST = SUPERS // 2
    LAG = PER + 4
    BEHIND = (BLOCKS - LAG) // 2
    PIECES = 8
    PERIOD = 2 * SUPERS
    EARLY = BLOCKS // (2 * SUPERS)
    LATE = SUPERS - EARLY
    SLOTS = 7

    def tri(i):
        return i * (i + 1) // 2

    LOW = tri(SUPERS)
    HIGH = LOW - SUPERS
    TILES1 = SUPERS * SUPERS
    PROD2 = LOW + HIGH
    TILE_OF = TILES1 - LOW
    TILE_LATE = TILE_OF - BEHIND

    def upper_tile(ii, gg):
        return ii * (SUPERS - 1) + gg - 1

    def lower_tile(ii, gg):
        return ii * (SUPERS - 1) + gg + (SUPERS - 1)

    def low_product(ii, gg):
        return tri(ii) + gg, (ii - 1) * (ii + 2) // 2 + gg, ii * (ii + 1) + gg * 2

    def high_product(k, j):
        return numbered((k - 1) * k // 2 + j + LOW)

    def high_half(k, j, h):
        return (k - 1) * k + j * 2 + h

    def high_column(k, j):
        gg = j + down(k) + 1
        return gg if isinstance(gg, int) else gg.with_bounds(min_val=0, max_val=SUPERS - 1)

    def numbered(m):
        return m, m - 1, m * 2

    def down(k):
        return k * -1 + (SUPERS - 1) if not isinstance(k, int) else SUPERS - 1 - k

    d_row = nc.dram_tensor("d_row", (BLOCKS, P), fp32).ap()
    sq_rows = nc.dram_tensor("sq_rows", (3, BLOCKS, P), bf16).ap()
    y2_rows = nc.dram_tensor("y2_rows", (N, F), fp32).ap()

    ctx = ExitStack()
    with ctx:
        def sb(name, shape, dt=fp32):
            return ctx.enter_context(nc.sbuf_tensor(name, shape, dt))

        def sem(name):
            return ctx.enter_context(nc.semaphore(name))

        base = (nc.sbuf_base + 31) // 32 * 32
        WORD, ROWS = 4, N * 4
        sb("arena", [P, 6 * N + 4 * HALF * F])

        def at(name, offset, shape, dt=fp32):
            return nc.alloc_sbuf_tensor_at(name, shape, dt, offset=base + offset)

        A, B, C, D, E = (i * ROWS for i in range(5))
        y1 = at("y1", A, [P, N])
        conv1_t = at("conv1_t", B, [P, N])
        ring = at("ring", C + 4 * SB * WORD, [P, SLOTS * HCOLS])
        lower_ring = at("lower_ring", C + 4 * SB * WORD, [P, 2 * HCOLS], fp32r)
        whole_ring = at("whole_ring", C + (4 * SB + 2 * HCOLS) * WORD, [P, 3 * HCOLS])
        upper_ring = at("upper_ring", C + (4 * SB + 5 * HCOLS) * WORD, [P, 2 * HCOLS], fp32r)
        works = [at(f"work{i}", C + i * SB * WORD, [P, SB]) for i in range(4)]
        partial, acc = works[0:2], works[2]
        lap_t, pre_z, z_sq, d_bcast = works
        scores = [at("scores_even", A, [P, N]), at("scores_odd", B, [P, N])]
        z_h = at("z_h", C, [P, N], fp32r)
        z_l = at("z_l", D, [P, N], fp32r)
        quarters = at("quarters", E, [P, HALF, SB])
        lower_quarters = at("lower_quarters", E, [P, HALF, SB], fp32r)
        y2_now = at("y2_now", E + HCOLS * WORD, [P, 2, HALF * F])
        y2_l = at("y2_l", E + HCOLS * WORD, [P, 2, HALF * F], fp32r)
        x_y2 = at("x_y2", E + (HCOLS + SB) * WORD, [P, SB])
        neg_half_sq = at("neg_half_sq", E + (HCOLS + 2 * SB) * WORD, [P, N // 4], bf16)
        z_stage_h = at("z_stage_h", E + (HCOLS + 3 * SB) * WORD, [P, 2, P], fp32r)
        z_stage_l = at("z_stage_l", E + (HCOLS + 3 * SB + 2 * P) * WORD, [P, 2, P], fp32r)
        conv2_t = at("conv2_t", E + ROWS, [P, N])
        y2_late = at("y2_late", A, [P, LATE * SB])
        near_sum, total_t, row_out, row_sq = (
            at(f"late{i}", A + (LATE + i) * SB * WORD, [P, SB]) for i in range(4))
        gathered = [at(f"gathered{i}", B + i * PER * K * F * WORD, [P, PER * K * F]) for i in range(2)]
        late_ring = at("late_ring", C, [P, 2 * 2 * HCOLS])
        y2_h = at("y2_h", 6 * ROWS, [P, 2, HALF * F], fp32r)
        upper_pieces = [at("upper_piece0", 6 * ROWS + SB * WORD, [P, BANK], fp32r),
                        at("upper_piece1", 6 * ROWS + (SB + BANK) * WORD, [P, BANK], fp32r),
                        at("upper_piece2", E + (HCOLS + 3 * SB + 4 * P) * WORD, [P, BANK], fp32r),
                        sb("upper_piece3", [P, BANK], fp32r)]
        y_stage = at("y_stage", 6 * ROWS + SB * WORD, [P, 2, HALF * F])
        y_stage_h = at("y_stage_h", 6 * ROWS + SB * WORD, [P, 2, HALF * F], fp32r)

        def ring_slot(tile, h, start=0, size=HCOLS):
            return ring[:, ds((tile * 2 + h) % SLOTS * HCOLS + start, size)]

        def whole_slot(v):
            return whole_ring[:, ds(v % 3 * HCOLS, HCOLS)]

        def upper_slot(v, start=0, size=HCOLS):
            return upper_ring[:, ds(v % 2 * HCOLS + start, size)]

        def lower_slot(v, start=0, size=HCOLS):
            return lower_ring[:, ds(v % 2 * HCOLS + start, size)]

        x_res = [y_stage[:, :, :].rearrange("p h n -> p (h n)"), x_y2[:, :]]
        y_stage_l = at("y_stage_l", 6 * ROWS, [P, 2, HALF * F], fp32r)
        rows_t = at("rows_t", 6 * ROWS, [BLOCKS, 3, P])
        rows_bf = at("rows_bf", 6 * ROWS + 3 * P * WORD, [BLOCKS, 3, P], bf16)
        ident = sb("ident", [P, P])
        ones = sb("ones", [P, 1])
        ones_bf = sb("ones_bf", [P, P], bf16)
        w1 = sb("w1", [F, F])
        w2 = sb("w2", [F, F])
        b1 = sb("b1", [F, 1])
        b2 = sb("b2", [P, F])
        row_sum = sb("row_sum", [P, BLOCKS])
        d1 = sb("d1", [P, BLOCKS])
        d2 = d1
        sq = sb("sq", [P, BLOCKS])
        best = sb("best", [P, BLOCKS, K])
        sim = best
        near = sb("near", [P, BLOCKS, K], u32)
        small = sb("small", [P, 4, PER])
        dist = sb("dist", [P, 2, PER, K])
        top = sb("top", [P, 2, 8])
        top_at = sb("top_at", [P, 2, 8], u32)
        gate = sb("gate", [P, 1])
        stat = sb("stat", [P, 4, PER])

        prod_ps = ctx.enter_context(nc.psum_tensor("prod_ps", [P, 2 * SB], fp32))
        score_ps = ctx.enter_context(nc.psum_tensor("score_ps", [P, 2 * SB], fp32))
        sums_ps = score_ps[:, 0:PER]
        z_ps = score_ps[:, SB:2 * SB]
        rows_ps = score_ps[0:BLOCKS, BANK:BANK + P]
        turned_ps = score_ps[:, 0:SB]
        dense_ps = score_ps[:, SB:2 * SB]

        s_const = sem("const_landed")
        s_x = sem("x_landed")
        s_memset = sem("constants_set")
        s_zeroed = sem("conv_zeroed")
        s_tile = [sem("tile_half0_landed"), sem("tile_half1_landed")]
        s_prod_half = sem("product_halves_done")
        s_staged = sem("y_halves_staged")
        s_added = sem("products_added")
        s_upper = sem("upper_halves_ready")
        s_upper_used = sem("upper_halves_multiplied")
        s_lower = sem("lower_halves_ready")
        s_ylow = sem("y_lower_halves_staged")
        s_partial = sem("partial_sums_ready")
        s_acc = sem("partial_sums_added")
        s_sums = sem("row_sums_in_psum")
        s_sums_c = sem("row_sums_copied")
        s_root = sem("roots_ready")
        s_d = sem("d_steps")
        s_y1 = sem("y1_supers_ready")
        s_dall = sem("d1_transposed")
        s_drows = sem("d_rows_copied")
        s_dstored = sem("d_row_stored")
        s_dbc = sem("d_broadcast_landed")
        s_lap = sem("lap_ready")
        s_zps = sem("z_in_psum")
        s_prez = sem("pre_z_ready")
        s_z = sem("z_supers_ready")
        s_zsq = sem("z_squares_ready")
        s_sqps = sem("sq_in_psum")
        s_sq = sem("sq_copied")
        s_zh = sem("z_upper_parts_ready")
        s_zl = sem("z_lower_parts_ready")
        s_y2now = [sem("y2_now_half0_landed"), sem("y2_now_half1_landed")]
        s_quarter = [sem(f"row_block{i}_landed") for i in range(4)]
        s_upiece = sem("upper_pieces_ready")
        s_lpiece = sem("lower_pieces_ready")
        s_piece = sem("pieces_multiplied")
        s_y2h = sem("y2_upper_halves_ready")
        s_y2l = sem("y2_lower_halves_ready")
        s_y2late = sem("y2_late_landed")
        s_sqt = sem("sq_transposed")
        s_split = sem("sq_split_steps")
        s_sqst = sem("sq_rows_stored")
        s_sqld = sem("sq_rows_landed")
        s_zst = sem("z_blocks_staged")
        s_chunk = sem("score_chunks_in_psum")
        s_evac = sem("score_chunks_copied")
        s_top = sem("tops_ready")
        s_at = sem("tops_located")
        s_kept = sem("tops_kept")
        s_dist = sem("distance_steps")
        s_exp = sem("similarity_steps")
        s_deg = sem("degree_steps")
        s_deg_root = sem("degree_roots_ready")
        s_y2 = sem("y2_supers_ready")
        s_y2st = sem("y2_stored")
        s_xg = sem("x_group_landed")
        s_gath = [sem("gathered_even"), sem("gathered_odd")]
        s_wgt = sem("gathered_weighted")
        s_nsum = sem("near_sums_ready")
        s_turn = sem("near_sums_turned")
        s_tot = sem("totals_ready")
        s_dense = sem("dense_in_psum")
        s_norm = sem("norm_steps")
        s_var = sem("variances_summed")
        s_nroot = sem("norm_roots_ready")
        s_done = sem("rows_done")
        s_xres = [sem("x_res_even"), sem("x_res_odd")]
        s_out = sem("out_stored")

        y2_view = y2_rows.rearrange("(s b p) f -> s p b f", b=PER, p=P)
        b2_row = b2_in.rearrange("(a f) -> a f", a=1)
        block = ctx.enter_context(nc.Block())

        @block.sync
        def _(sp):
            sp.dma_start(y1[:, :], x_in).then_inc(s_x, 16)

            def load_half(tile, ii, gg, h, to, free):
                for s, v in free:
                    sp.wait_ge(s, v)
                if not (isinstance(tile, int) and tile == 0):
                    sp.wait_ge(s_tile[h], tile * 16)
                sp.dma_start(to, adj_in[ds((ii * SUPERS + gg) * 2 + h, 1), :, :].rearrange("a p n -> p (a n)")
                             ).then_inc(s_tile[h], 16)

            def halves_multiplied(u):
                ii, pos = u // (2 * SUPERS), u // 2 % SUPERS
                gg = pos - (SUPERS - 1 - ii)
                return 2 * (tri(ii) + gg) + u % 2 + 1 if gg >= 0 else 2 * tri(ii)

            for n in range(TILES1):
                ii, pos = n // SUPERS, n % SUPERS
                for h in range(2):
                    before = n * 2 + h - SLOTS
                    free = [(s_partial, before + 1)] if before >= 0 else []
                    if before >= 0 and halves_multiplied(before) > 0:
                        free.append((s_prod_half, halves_multiplied(before)))
                    load_half(n, ii, (ii + 1 + pos) % SUPERS, h, ring_slot(n, h), free)


            def load_high(k, j):
                m = high_product(k, j)[0]
                for h in range(2):
                    v = high_half(k, j, h)
                    if isinstance(v, int) and v < 3:
                        free = [(s_prod_half, v + (2 * LOW - SLOTS + 1)), (s_partial, v + (2 * TILES1 - SLOTS + 1))]
                    else:
                        free = [(s_lower, v - 2)]
                    load_half(m + TILE_OF, down(k), high_column(k, j), h, whole_slot(v), free)

            load_high(1, 0)
            load_high(2, 0)
            load_high(2, 1)
            with sp.Fori(3, SUPERS) as k:
                with sp.Fori(0, k) as j:
                    load_high(k, j)

            sp.wait_ge(s_split, 5)
            sp.dma_start(sq_rows.rearrange("r b p -> b r p"), rows_bf[:, :, :]).then_inc(s_sqst, 16)
            sp.wait_ge(s_sqst, 16)
            sp.wait_ge(s_prod_half, 2 * PROD2)
            sq_flat = sq_rows.rearrange("r (q g b) p -> g r q (b p)", g=4, b=BANK // P)
            for g in range(4):
                sp.dma_start(neg_half_sq[32 * g:32 * g + 3, :].rearrange("r (q c) -> r q c", c=BANK),
                             sq_flat[g]).then_inc(s_sqld, 16)

            def load_group(g):
                sp.dma_start(x_y2[:, :], x_in[:, ds(g * SB, SB)]).then_inc(s_xg, 16)

            def store_group(g):
                sp.wait_ge(s_y2, g + 1)
                sp.dma_start(y2_view[ds(g, 1), :, :, :].rearrange("a p b f -> p (a b) f"),
                             x_y2[:, :].rearrange("p (b f) -> p b f", f=F)).then_inc(s_y2st, 16)

            def next_group(g):
                sp.wait_ge(s_y2st, g * 16)
                load_group(g)

            def load_y2(gg, h):
                sp.dma_start(y2_now[:, h, :].rearrange("p (b f) -> p b f", f=F),
                             y2_view[ds(gg, 1), :, h * HALF:(h + 1) * HALF, :].rearrange("a p b f -> p (a b) f")
                             ).then_inc(s_y2now[h], 16)

            def load_quarters(w, gg, h):
                for b in range(HALF):
                    if not (isinstance(w, int) and w == 0):
                        sp.wait_ge(s_piece, w * PIECES + 2 * b - 6)
                    half = (w - gg * PERIOD) * SUPERS - h * (SUPERS - 1) + gg * 2
                    if not isinstance(half, int):
                        half = half.with_bounds(min_val=0, max_val=2 * TILES1 - 1)
                    source = adj_in[ds(half, 1), :, b * SB:(b + 1) * SB]
                    sp.dma_start(quarters[:, b, :], source.rearrange("a p n -> p (a n)")
                                 ).then_inc(s_quarter[b], 16)

            load_group(0)
            store_group(0)
            next_group(1)
            load_y2(0, 0)
            load_y2(0, 1)
            load_quarters(0, 0, 0)
            for gg in range(EARLY - 1):
                start = gg * PERIOD
                load_quarters(start + 1, gg, 1)
                for g in (2 * gg, 2 * gg + 1):
                    if g > 0:
                        store_group(g)
                        next_group(g + 1)
                    with sp.Fori(g * SUPERS // 2 + 1, g * SUPERS // 2 + (SUPERS - 2) // 2) as q:
                        for h in range(2):
                            load_quarters(q * 2 + h, gg, h)
                    end = (g + 1) * SUPERS
                    load_quarters(end - 2, gg, 0)
                    load_quarters(end - 1, gg, 1)
                    if g == 2 * gg:
                        load_quarters(end, gg, 0)
                        load_quarters(end + 1, gg, 1)
                    else:
                        load_y2(gg + 1, 0)
                        load_quarters(end, gg + 1, 0)
                        load_y2(gg + 1, 1)
            gg = EARLY - 1
            load_quarters(gg * PERIOD + 1, gg, 1)
            store_group(2 * gg)
            next_group(2 * gg + 1)
            with sp.Fori(gg * SUPERS + 1, BEHIND) as q:
                for h in range(2):
                    load_quarters(q * 2 + h, gg, h)

            sp.wait_ge(s_piece, 2 * BEHIND * PIECES)
            sp.dma_start(y2_now[:, :, :].rearrange("p h (b f) -> p (h b) f", f=F),
                         y2_view[EARLY - 1:EARLY, :, :, :].rearrange("a p b f -> p (a b) f")).then_inc(s_y2now[0], 16)
            def late_half(m, ii, gg, h, slot_no):
                load_half(m + TILE_LATE, ii, gg, h, late_ring[:, ds(slot_no * (2 * HCOLS) + h * HCOLS, HCOLS)],
                          [(s_prod_half, m * 2 - 3 + h - 2 * BEHIND)])

            sp.wait_ge(s_chunk, BLOCKS * PER)
            with sp.Fori(BEHIND % SUPERS, SUPERS) as ii:
                m = ii + (PROD2 + (EARLY - 1) * SUPERS)
                for h in range(2):
                    late_half(m, ii, EARLY - 1, h, m % 2)

            store_group(SUPERS - 1)
            sp.wait_ge(s_y2st, 16 * SUPERS)
            sp.wait_ge(s_kept, 2 * BLOCKS)
            sp.dma_start(y2_late[:, :].rearrange("p (s b f) -> p s b f", f=F, b=PER),
                         y2_view[EARLY:SUPERS].rearrange("s p b f -> p s b f")).then_inc(s_y2late, 16)

            def late_tile(ii, j):
                for h in range(2):
                    late_half(ii * LATE + j + (PROD2 + EARLY * SUPERS), ii, EARLY + j, h, j % 2)

            def load_x(g, p):
                sp.dma_start(x_res[p], x_in[:, ds(g * SB, SB)]).then_inc(s_xres[p], 16)

            def store(g):
                sp.wait_ge(s_done, g + 1)
                sp.dma_start(out[:, ds(g * SB, SB)], row_out[:, :]).then_inc(s_out, 16)

            load_x(0, 0)
            load_x(1, 1)
            with sp.Fori(0, 2) as ii:
                for j in range(LATE):
                    late_tile(ii, j)
            with sp.Fori(1, SUPERS // 2) as q:
                for p in range(2):
                    for j in range(LATE):
                        late_tile(q * 2 + p, j)
                        if j == 0:
                            store(q * 2 + p - 2)
                            load_x(q * 2 + p, p)
            store(SUPERS - 2)
            store(SUPERS - 1)
            sp.wait_ge(s_out, 16 * SUPERS)

        @block.gpsimd
        def _(pool):
            pool.dma_start(w1[:, :], w1_in).then_inc(s_const, 16)
            pool.dma_start(w2[:, :], w2_in).then_inc(s_const, 16)
            pool.dma_start(b1[:, :], b1_in.rearrange("(f a) -> f a", a=1)).then_inc(s_const, 16)
            pool.dma_start(b2[:, :], b2_row.to_broadcast([P, F])).then_inc(s_const, 16)
            nc.gpsimd.memset(ident[:, :], 0.0).then_inc(s_memset, 1)
            pool.wait_ge(s_memset, 1)
            nc.gpsimd.affine_select(out=ident[:, :], in_=ident[:, :], compare_op=ALU.not_equal, fill=1.0, base=0,
                                    pattern=[[-1, P]], channel_multiplier=1).then_inc(s_memset, 1)
            nc.gpsimd.memset(ones[:, :], 1.0).then_inc(s_memset, 1)
            nc.gpsimd.memset(ones_bf[:, :], 1.0).then_inc(s_memset, 1)
            nc.gpsimd.memset(conv1_t[:, :], 0.0).then_inc(s_zeroed, 1)

            def add_partial(count, h):
                pool.wait_ge(s_partial, count + 1)
                pool.wait_ge(s_acc, count)
                nc.gpsimd.tensor_tensor(acc[:, :], acc[:, :], partial[h][:, :], ALU.add).then_inc(s_acc, 1)

            with pool.Fori(0, SUPERS) as ii:
                pool.wait_ge(s_sums, ii)
                pool.wait_ge(s_partial, ii * (2 * SUPERS) + 2)
                nc.gpsimd.tensor_tensor(acc[:, :], partial[0][:, :], partial[1][:, :], ALU.add).then_inc(s_acc, 2)
                with pool.Fori(1, SUPERS) as k:
                    for h in range(2):
                        add_partial((ii * SUPERS + k) * 2 + h, h)

            pool.wait_ge(s_drows, 1)
            pool.dma_start(d_row, rows_t[:, 0, :]).then_inc(s_dstored, 16)
            pool.wait_ge(s_dstored, 16)
            d_flat = d_row.rearrange("(s b) p -> s (b p)", b=PER)

            def load_d(k):
                if not (isinstance(k, int) and k == 0):
                    pool.wait_ge(s_lap, k)
                pool.dma_start(d_bcast[:, :], d_flat[ds(down(k), 1), :].to_broadcast([P, SB])).then_inc(s_dbc, 16)

            def lower_y(k, j):
                for h in range(2):
                    pool.wait_ge(s_staged, high_half(k, j, h) + (2 * LOW + 1))
                    nc.gpsimd.tensor_tensor(
                        y_stage_l[:, h, :], y1[:, ds(high_column(k, j) * (PER * F) + h * (HALF * F), HALF * F)],
                        y_stage_h[:, h, :].bitcast(fp32), ALU.subtract).then_inc(s_ylow, 1)

            load_d(0)
            lower_y(1, 0)
            load_d(1)
            for j in range(2):
                lower_y(2, j)
            load_d(2)
            with pool.Fori(3, SUPERS) as k:
                for j in range(2):
                    lower_y(k, j)
                load_d(k)
                with pool.Fori(2, k) as j:
                    lower_y(k, j)

            pool.wait_ge(s_prod_half, 2 * PROD2)
            nc.gpsimd.memset(conv2_t[:, :], 0.0).then_inc(s_zeroed, 1)

            def lower_pieces(w):
                for i in range(PIECES):
                    b, at_c = i // 2, ds(i % 2 * BANK, BANK)
                    pool.wait_ge(s_upiece, w * PIECES + i + 1)
                    nc.gpsimd.tensor_tensor(lower_quarters[:, b, at_c], quarters[:, b, at_c],
                                            upper_pieces[i % 4][:, :].bitcast(fp32), ALU.subtract
                                            ).then_inc(s_lpiece, 1)

            def lower_y2(gg, h):
                pool.wait_ge(s_y2h, gg * 2 + h + 1)
                nc.gpsimd.tensor_tensor(y2_l[:, h, :], y2_now[:, h, :], y2_h[:, h, :].bitcast(fp32),
                                        ALU.subtract).then_inc(s_y2l, 1)

            lower_y2(0, 0)
            lower_y2(0, 1)
            lower_pieces(0)
            with pool.Fori(1, EARLY) as gg:
                with pool.Fori(1, PERIOD) as w:
                    lower_pieces(w + (gg - 1) * PERIOD)
                lower_y2(gg, 0)
                lower_pieces(gg * PERIOD)
                lower_y2(gg, 1)
            with pool.Fori((EARLY - 1) * PERIOD + 1, 2 * BEHIND) as w:
                lower_pieces(w)

            pool.wait_ge(s_kept, 2 * BLOCKS)
            pool.wait_ge(s_y2st, 16 * SUPERS)
            for g in range(SUPERS):
                if g >= 2:
                    pool.wait_ge(s_nsum, g - 1)
                for j in range(PER * K):
                    nc.gpsimd.indirect_dma_start(
                        gathered[g % 2][:, j * F:(j + 1) * F], None, y2_rows,
                        bass.IndirectOffsetOnAxis(ap=near[:, g * PER + j // K, j % K:j % K + 1], axis=0)
                    ).then_inc(s_gath[g % 2], 16)

        @block.scalar
        def _(act):
            def stage_y(product, gg, ready):
                act.wait_ge(s_y1, ready)
                for h in range(2):
                    if not (isinstance(product[0], int) and product[0] == 0):
                        act.wait_ge(s_prod_half, product[2] - 1 + h)
                    nc.scalar.copy(y_stage[:, h, :], y1[:, ds(gg * (PER * F) + h * (HALF * F), HALF * F)]
                                   ).then_inc(s_staged, 1)

            def root(ii):
                act.wait_ge(s_sums_c, ii + 1)
                nc.scalar.activation(small[:, 1, :], small[:, 0, :], ACT.Sqrt).then_inc(s_root, 1)

            root(0)
            stage_y(low_product(0, 0), 0, 1)
            with act.Fori(1, SUPERS) as ii:
                with act.Fori(0, ii) as gg:
                    stage_y(low_product(ii, gg), gg, 1)
                root(ii)
                stage_y(low_product(ii, ii), ii, ii + 1)

            def pre_activation(k):
                act.wait_ge(s_zps, k + 1)
                nc.scalar.activation(pre_z[:, :], z_ps, ACT.Identity, bias=b1[:, 0:1]).then_inc(s_prez, 1)

            def square(k):
                act.wait_ge(s_z, k + 1)
                nc.scalar.activation(z_sq[:, :], conv1_t[:, ds(down(k) * SB, SB)], ACT.Square).then_inc(s_zsq, 1)

            def upper_y(k, j, h):
                act.wait_ge(s_prod_half, high_half(k, j, h) + (2 * LOW - 1))
                nc.scalar.copy(y_stage_h[:, h, :], y1[:, ds(high_column(k, j) * (PER * F) + h * (HALF * F), HALF * F)]
                               ).then_inc(s_staged, 1)

            def upper_tile_half(k, j, h):
                v = high_half(k, j, h)
                if isinstance(v, int) and v < 2:
                    act.wait_ge(s_prod_half, v + (2 * LOW - 3))
                else:
                    act.wait_ge(s_upper_used, v - 1)
                    act.wait_ge(s_lower, v - 1)
                act.wait_ge(s_tile[h], high_product(k, j)[0] * 16 + (TILE_OF * 16 + 16))
                nc.scalar.copy(upper_slot(v), whole_slot(v)).then_inc(s_upper, 1)

            def upper_parts(k, j, after):
                upper_y(k, j, 0)
                upper_tile_half(k, j, 1)
                upper_y(k, j, 1)
                if after is not None:
                    upper_tile_half(after[0], after[1], 0)

            def upper_z(c):
                nc.scalar.copy(z_h[:, c * SB:(c + 1) * SB], conv1_t[:, c * SB:(c + 1) * SB]).then_inc(s_zh, 1)

            upper_tile_half(1, 0, 0)
            upper_parts(1, 0, (2, 0))
            pre_activation(0)
            upper_parts(2, 0, (2, 1))
            square(0)
            pre_activation(1)
            upper_parts(2, 1, (3, 0))
            square(1)
            with act.Fori(3, SUPERS - 1) as k:
                upper_parts(k, 0, (k, 1))
                pre_activation(k - 1)
                with act.Fori(1, k - 1) as j:
                    upper_parts(k, j, (k, j + 1))
                upper_parts(k, k - 1, (k + 1, 0))
                square(k - 1)
            last = SUPERS - 1
            upper_parts(last, 0, (last, 1))
            pre_activation(last - 1)
            with act.Fori(1, last - 1) as j:
                upper_parts(last, j, (last, j + 1))
            upper_parts(last, last - 1, None)
            square(last - 1)
            act.wait_ge(s_prod_half, 2 * PROD2)
            for c in range(SPLIT_FIRST, SUPERS):
                upper_z(c)
            pre_activation(last)
            square(last)
            act.wait_ge(s_sqps, SUPERS)
            for c in range(SPLIT_FIRST):
                upper_z(c)

            def upper_piece(w, i):
                if i % 2 == 0:
                    act.wait_ge(s_quarter[i // 2], w * 16 + 16)
                if not (isinstance(w, int) and w * PIECES + i < 4):
                    act.wait_ge(s_piece, w * PIECES + i - 3)
                nc.scalar.copy(upper_pieces[i % 4][:, :], quarters[:, i // 2, i % 2 * BANK:(i % 2 + 1) * BANK]
                               ).then_inc(s_upiece, 1)

            def upper_y2(gg, h):
                act.wait_ge(s_y2now[h], gg * 16 + 16)
                nc.scalar.copy(y2_h[:, h, :], y2_now[:, h, :]).then_inc(s_y2h, 1)

            def stage_z(t, p):
                nc.scalar.copy(z_stage_h[:, p, :], z_h[:, ds(t * P, P)].bitcast(fp32))
                nc.scalar.copy(z_stage_l[:, p, :], z_l[:, ds(t * P, P)].bitcast(fp32)).then_inc(s_zst, 1)

            def search(t, p, first=False, w=None, y2=None, last=False):
                if not first:
                    act.wait_ge(s_at, t - 1)
                for c in range(PER):
                    act.wait_ge(s_chunk, t * PER + c + 1)
                    nc.scalar.copy(scores[p][:, c * SB:(c + 1) * SB],
                                   score_ps[:, (c % 2) * SB:(c % 2 + 1) * SB]).then_inc(s_evac, 1)
                    if c == 1 and not last:
                        stage_z(t + 1, 1 - p)
                    if w is not None and not (last and c >= PIECES - 2):
                        upper_piece(w + (c + 2) // PIECES, (c + 2) % PIECES)
                    if y2 is not None and c == PIECES // 2:
                        upper_y2(*y2)

            def searches(w, y2=None, last=False):
                for p in range(2):
                    search(w + LAG + p, p, w=w + p, y2=y2 if p else None, last=last and p == 1)

            def similarities(g):
                act.wait_ge(s_dist, g * 2 + 2)
                nc.scalar.activation(dist[:, 0], dist[:, 0], ACT.Sqrt).then_inc(s_exp, 1)
                act.wait_ge(s_exp, g * 2 + 1)
                nc.scalar.activation(dist[:, 1], dist[:, 0], ACT.Exp, scale=-0.5).then_inc(s_exp, 1)
                act.wait_ge(s_deg, g * 4 + 2)
                nc.scalar.activation(small[:, 1, :], small[:, 0, :], ACT.Sqrt).then_inc(s_deg_root, 1)

            act.wait_ge(s_zl, SUPERS)
            act.wait_ge(s_prod_half, 2 * PROD2)
            stage_z(0, 0)
            search(0, 0, True)
            search(1, 1, True)
            with act.Fori(1, PER // 2 + 1) as q:
                for p in range(2):
                    search(q * 2 + p, p)
            similarities(0)
            with act.Fori(PER // 2 + 1, LAG // 2) as q:
                for p in range(2):
                    search(q * 2 + p, p)
            upper_y2(0, 0)
            upper_y2(0, 1)
            upper_piece(0, 0)
            upper_piece(0, 1)
            search(LAG, 0, w=0)
            search(LAG + 1, 1, w=1)
            with act.Fori(0, EARLY - 1) as n:
                for g in range(2):
                    start = n * PERIOD + g * SUPERS
                    with act.Fori(1, 3) as q:
                        searches(start + q * 2)
                    similarities(n * 2 + g + 1)
                    if g == 0:
                        searches(start + 6)
                        searches(start + 8)
                searches(n * PERIOD + PERIOD - 2, y2=(n + 1, 0))
                search(n * PERIOD + (PERIOD + LAG), 0, w=n * PERIOD + PERIOD, y2=(n + 1, 1))
                search(n * PERIOD + (PERIOD + LAG + 1), 1, w=n * PERIOD + (PERIOD + 1))
            searches(2 * BEHIND - 2, last=True)
            similarities(SUPERS - 1)

            with act.Fori(0, SUPERS) as g:
                act.wait_ge(s_norm, g * 8 + 7)
                nc.scalar.activation(stat[:, 2, :], stat[:, 1, :], ACT.Sqrt).then_inc(s_nroot, 1)

        @block.vector
        def _(dve):
            def sum_tile(n):
                for h in range(2):
                    dve.wait_ge(s_tile[h], n * 16 + 16)
                    if not (isinstance(n, int) and n == 0):
                        dve.wait_ge(s_acc, n * 2 - 1 + h)
                    nc.vector.tensor_reduce(
                        partial[h][:, :],
                        ring_slot(n, h).rearrange("p (b i) -> p i b", b=HALF),
                        X, ALU.add).then_inc(s_partial, 1)

            def add_product(product, target, at):
                m, _, halves = product
                dve.wait_ge(s_prod_half, halves + 2)
                dve.wait_ge(s_added, m)
                nc.vector.tensor_tensor(target[:, ds(at, SB)], target[:, ds(at, SB)],
                                        prod_ps[:, ds((m % 2) * SB, SB)], ALU.add).then_inc(s_added, 1)

            def finish_rows(ii):
                dve.wait_ge(s_sums, ii + 1)
                nc.vector.tensor_copy(small[:, 0, :], sums_ps).then_inc(s_sums_c, 1)
                nc.vector.tensor_copy(row_sum[:, ds(ii * PER, PER)], sums_ps)
                dve.wait_ge(s_root, ii + 1)
                nc.vector.reciprocal(small[:, 2, :], small[:, 1, :]).then_inc(s_d, 1)
                dve.wait_ge(s_d, ii * 2 + 1)
                nc.vector.tensor_copy(d1[:, ds(ii * PER, PER)], small[:, 2, :]).then_inc(s_d, 1)
                v = y1[:, ds(ii * SB, SB)].rearrange("p (b f) -> p b f", f=F)
                nc.vector.tensor_tensor(v, v, small[:, 2, :].unsqueeze(2).to_broadcast([P, PER, F]),
                                        ALU.mult).then_inc(s_y1, 1)

            dve.wait_ge(s_x, 16)
            for n in range(SUPERS):
                sum_tile(n)
            finish_rows(0)
            dve.wait_ge(s_zeroed, 1)

            def sum_row(ii, upper, longer):
                if upper:
                    with dve.Fori(ii + 1, SUPERS) as gg:
                        sum_tile(upper_tile(ii, gg))
                add_product(low_product(ii - 1, ii - 1), conv1_t, ii * SB - SB)
                sum_tile(lower_tile(ii, 0))
                if longer:
                    with dve.Fori(1, ii) as gg:
                        sum_tile(lower_tile(ii, gg))
                        add_product(low_product(ii, gg - 1), conv1_t, ii * SB)
                sum_tile(lower_tile(ii, ii))
                finish_rows(ii)
                add_product(low_product(ii, ii - 1), conv1_t, ii * SB)

            sum_row(1, True, False)
            with dve.Fori(2, LATE_ROW) as ii:
                sum_row(ii, True, True)
            for ii in range(LATE_ROW, SUPERS):
                if ii < SUPERS - 1:
                    with dve.Fori(ii + 1, SUPERS) as gg:
                        sum_tile(upper_tile(ii, gg))
                add_product(low_product(ii - 1, ii - 1), conv1_t, ii * SB - SB)
                sum_tile(lower_tile(ii, 0))
                with dve.Fori(1, ii - 1) as gg:
                    sum_tile(lower_tile(ii, gg))
                    add_product(low_product(ii, gg - 1), conv1_t, ii * SB)
                sum_tile(lower_tile(ii, ii - 1))
                sum_tile(lower_tile(ii, ii))
                add_product(low_product(ii, ii - 2), conv1_t, ii * SB)
                finish_rows(ii)
                add_product(low_product(ii, ii - 1), conv1_t, ii * SB)
            last = SUPERS - 1
            dve.wait_ge(s_dall, 1)
            nc.vector.tensor_copy(rows_t[:, 0, :], rows_ps).then_inc(s_drows, 1)
            add_product(numbered(LOW - 1), conv1_t, last * SB)

            def lap(k, added):
                dve.wait_ge(s_dbc, k * 16 + 16)
                dve.wait_ge(s_added, added)
                if not (isinstance(k, int) and k == 0):
                    dve.wait_ge(s_zps, k)
                nc.vector.tensor_tensor(lap_t[:, :], conv1_t[:, ds(down(k) * SB, SB)], d_bcast[:, :],
                                        ALU.mult).then_inc(s_lap, 1)

            def leaky(k):
                dve.wait_ge(s_prez, k + 1)
                nc.vector.scalar_tensor_tensor(conv1_t[:, ds(down(k) * SB, SB)], pre_z[:, :], 0.1, pre_z[:, :],
                                               ALU.mult, ALU.max).then_inc(s_z, 1)

            def copy_sq(k):
                dve.wait_ge(s_sqps, k + 1)
                nc.vector.tensor_copy(sq[:, ds(down(k) * PER, PER)], sums_ps).then_inc(s_sq, 1)

            def lower_tile_parts(k, j):
                for h in range(2):
                    v = high_half(k, j, h)
                    dve.wait_ge(s_upper, v + 1)
                    dve.wait_ge(s_prod_half, v + (2 * LOW - 1))
                    nc.vector.tensor_tensor(lower_slot(v), whole_slot(v), upper_slot(v).bitcast(fp32),
                                            ALU.subtract).then_inc(s_lower, 1)

            lower_tile_parts(1, 0)
            lap(0, LOW)
            leaky(0)
            lower_tile_parts(2, 0)
            add_product(high_product(1, 0), conv1_t, down(1) * SB)
            lap(1, high_product(2, 0)[0])
            lower_tile_parts(2, 1)
            add_product(high_product(2, 0), conv1_t, down(2) * SB)
            leaky(1)
            copy_sq(0)
            with dve.Fori(3, SUPERS) as k:
                lower_tile_parts(k, 0)
                add_product(high_product(k - 1, k - 2), conv1_t, down(k - 1) * SB)
                copy_sq(k - 2)
                lap(k - 1, high_product(k, 0)[0])
                lower_tile_parts(k, 1)
                add_product(high_product(k, 0), conv1_t, down(k) * SB)
                leaky(k - 1)
                with dve.Fori(2, k) as j:
                    lower_tile_parts(k, j)
                    add_product(high_product(k, j - 1), conv1_t, down(k) * SB)
            add_product(high_product(last, last - 1), conv1_t, 0)
            copy_sq(last - 1)
            lap(last, PROD2)

            def lower_z(count, c):
                dve.wait_ge(s_zh, count + 1)
                nc.vector.tensor_tensor(z_l[:, c * SB:(c + 1) * SB], conv1_t[:, c * SB:(c + 1) * SB],
                                        z_h[:, c * SB:(c + 1) * SB].bitcast(fp32), ALU.subtract).then_inc(s_zl, 1)

            split_order = [*range(SPLIT_FIRST, SUPERS), *range(SPLIT_FIRST)]
            for count in range(2):
                lower_z(count, split_order[count])
            leaky(last)
            for count in range(2, 4):
                lower_z(count, split_order[count])
            copy_sq(last)

            dve.wait_ge(s_sqt, 1)
            nc.vector.tensor_scalar(rows_t[:, 1, :], rows_ps, -0.5, None, ALU.mult).then_inc(s_split, 1)
            dve.wait_ge(s_split, 1)
            nc.vector.tensor_copy(rows_bf[:, 0, :], rows_t[:, 1, :]).then_inc(s_split, 1)
            dve.wait_ge(s_split, 2)
            nc.vector.tensor_tensor(rows_t[:, 2, :], rows_t[:, 1, :], rows_bf[:, 0, :],
                                    ALU.subtract).then_inc(s_split, 1)
            dve.wait_ge(s_split, 3)
            nc.vector.tensor_copy(rows_bf[:, 1, :], rows_t[:, 2, :]).then_inc(s_split, 1)
            dve.wait_ge(s_split, 4)
            nc.vector.tensor_tensor(rows_bf[:, 2, :], rows_t[:, 2, :], rows_bf[:, 1, :],
                                    ALU.subtract).then_inc(s_split, 1)

            for count in range(4, SUPERS):
                lower_z(count, split_order[count])

            def search(t, p):
                dve.wait_ge(s_evac, t * PER + PER)
                nc.vector.tensor_copy(gate[:, 0:1], ones[:, :])
                nc.vector.max(top[:, p, :], scores[p][:, :]).then_inc(s_top, 1)
                dve.wait_ge(s_top, t + 1)
                nc.vector.tensor_copy(best[:, ds(t, 1), :].rearrange("p a k -> p (a k)"),
                                      top[:, p, 0:K]).then_inc(s_kept, 1)
                nc.vector.max_index(top_at[:, p, :], top[:, p, :], scores[p][:, :]).then_inc(s_at, 1)
                dve.wait_ge(s_at, t + 1)
                nc.vector.tensor_copy(near[:, ds(t, 1), :].rearrange("p a k -> p (a k)"),
                                      top_at[:, p, 0:K]).then_inc(s_kept, 1)

            def follow(pair, late=False):
                u = pair - LAG // 2
                m, before, _ = numbered(u + PROD2)
                if late:
                    dve.wait_ge(s_prod_half, m * 2 + (2 - 2 * BEHIND))
                else:
                    dve.wait_ge(s_piece, u * (2 * PIECES) + 2 * PIECES)
                dve.wait_ge(s_added, m)
                target = conv2_t[:, ds((u % SUPERS) * SB, SB)]
                nc.vector.tensor_tensor(target, target, prod_ps[:, ds((m % 2) * SB, SB)], ALU.add
                                        ).then_inc(s_added, 1)

            def new_degrees(g, kept):
                at = ds(g * PER, PER)
                dve.wait_ge(s_kept, kept)
                nc.vector.scalar_tensor_tensor(dist[:, 0], best[:, at, :], -2.0,
                                               sq[:, at].unsqueeze(2).to_broadcast([P, PER, K]),
                                               ALU.mult, ALU.add).then_inc(s_dist, 1)
                dve.wait_ge(s_dist, g * 2 + 1)
                nc.vector.tensor_scalar(dist[:, 0], dist[:, 0], 0.0, EPS_DIST, ALU.max, ALU.add).then_inc(s_dist, 1)
                dve.wait_ge(s_exp, g * 2 + 2)
                nc.vector.tensor_reduce(small[:, 3, :], dist[:, 1], X, ALU.add).then_inc(s_deg, 1)
                nc.vector.tensor_copy(sim[:, at, :], dist[:, 1])
                dve.wait_ge(s_deg, g * 4 + 1)
                nc.vector.tensor_tensor(small[:, 0, :], small[:, 3, :], row_sum[:, at], ALU.add).then_inc(s_deg, 1)
                dve.wait_ge(s_deg_root, g + 1)
                nc.vector.reciprocal(small[:, 2, :], small[:, 1, :]).then_inc(s_deg, 1)
                dve.wait_ge(s_deg, g * 4 + 3)
                nc.vector.tensor_copy(d2[:, at], small[:, 2, :]).then_inc(s_deg, 1)
                dve.wait_ge(s_xg, g * 16 + 16)
                v = x_y2[:, :].rearrange("p (b f) -> p b f", f=F)
                nc.vector.tensor_tensor(v, v, small[:, 2, :].unsqueeze(2).to_broadcast([P, PER, F]),
                                        ALU.mult).then_inc(s_y2, 1)

            def segment(g, with_products, first=0):
                with dve.Fori(first, PER // 2 - 1) as q:
                    for p in range(2):
                        search(g * PER + q * 2 + 2 + p, p)
                    if with_products:
                        follow(g * (PER // 2) + q + 1)
                search(g * PER + PER, 0)
                new_degrees(g, (g * PER + PER + 1) * 2)
                search(g * PER + PER + 1, 1)
                if with_products:
                    follow(g * (PER // 2) + PER // 2)

            search(0, 0)
            search(1, 1)
            segment(0, False)
            dve.wait_ge(s_zeroed, 2)
            search(PER + 2, 0)
            search(PER + 3, 1)
            segment(1, True, 1)
            with dve.Fori(2, SUPERS - 1) as g:
                segment(g, True)
            with dve.Fori((BLOCKS - PER) // 2 + 1, BLOCKS // 2) as pair:
                search(pair * 2, 0)
                search(pair * 2 + 1, 1)
                follow(pair)
            new_degrees(SUPERS - 1, 2 * BLOCKS)
            with dve.Fori(BLOCKS // 2, EARLY * SUPERS + LAG // 2) as pair:
                follow(pair, True)

            def late_sums(g, q, p):
                rows = gathered[p][:, :].rearrange("p (b k f) -> p b k f", k=K, f=F)
                dve.wait_ge(s_gath[p], (q + 1) * (16 * PER * K))
                for b in range(PER):
                    w = nc.vector.tensor_tensor(
                        rows[:, b], rows[:, b],
                        sim[:, ds(g * PER + b, 1), :].rearrange("p a k -> p (a k)").unsqueeze(2).to_broadcast([P, K, F]),
                        ALU.mult)
                w.then_inc(s_wgt, 1)
                dve.wait_ge(s_wgt, g + 1)
                if not (isinstance(g, int) and g == 0):
                    dve.wait_ge(s_turn, g)
                nc.vector.tensor_reduce(near_sum[:, :].rearrange("p (b f) -> p b f", f=F),
                                        rows.rearrange("p b k f -> p b f k"), X, ALU.add).then_inc(s_nsum, 1)

            def totals(g):
                dve.wait_ge(s_prod_half, g * (2 * LATE) + 2 * (PROD2 + EARLY * SUPERS + LATE - BEHIND))
                nc.vector.tensor_tensor(conv2_t[:, ds(g * SB, SB)], conv2_t[:, ds(g * SB, SB)],
                                        prod_ps[:, ds((g % 2) * SB, SB)], ALU.add).then_inc(s_added, 1)
                dve.wait_ge(s_added, g + (PROD2 + EARLY * SUPERS + 1))
                dve.wait_ge(s_turn, g + 1)
                if not (isinstance(g, int) and g == 0):
                    dve.wait_ge(s_dense, g)
                nc.vector.tensor_tensor(total_t[:, :], turned_ps, conv2_t[:, ds(g * SB, SB)],
                                        ALU.add).then_inc(s_tot, 1)

            def finish(g, q, p):
                at = ds(g * PER, PER)
                out3 = row_out[:, :].rearrange("p (b f) -> p b f", f=F)
                sq3 = row_sq[:, :].rearrange("p (b f) -> p b f", f=F)
                n = [0]

                def step(ins):
                    n[0] += 1
                    ins.then_inc(s_norm, 1)
                    dve.wait_ge(s_norm, g * 8 + n[0])

                x3 = x_res[p][:, :].rearrange("p (b f) -> p b f", f=F)
                dve.wait_ge(s_xres[p], q * 16 + 16)
                nc.vector.tensor_tensor(x3, x3, b2[:, :].unsqueeze(1).to_broadcast([P, PER, F]), ALU.add
                                        ).then_inc(s_norm, 1)
                n[0] = 1
                dve.wait_ge(s_dense, g + 1)
                if not (isinstance(g, int) and g == 0):
                    dve.wait_ge(s_out, g * 16)
                step(nc.vector.tensor_tensor(out3, dense_ps.rearrange("p (b f) -> p b f", f=F),
                                             d2[:, at].unsqueeze(2).to_broadcast([P, PER, F]), ALU.mult))
                step(nc.vector.tensor_tensor(row_out[:, :], row_out[:, :], x_res[p][:, :], ALU.add))
                step(nc.vector.tensor_reduce(stat[:, 0, :], out3, X, ALU.add))
                nc.vector.scalar_tensor_tensor(out3, stat[:, 0, :].unsqueeze(2).to_broadcast([P, PER, F]), -1.0 / F,
                                               out3, ALU.mult, ALU.add).then_inc(s_norm, 1)
                dve.wait_ge(s_norm, g * 8 + 5)
                nc.vector.tensor_tensor(row_sq[:, :], row_out[:, :], row_out[:, :], ALU.mult).then_inc(s_norm, 1)
                dve.wait_ge(s_norm, g * 8 + 6)
                nc.vector.tensor_reduce(stat[:, 0, :], sq3, X, ALU.add).then_inc(s_var, 1)
                dve.wait_ge(s_var, g + 1)
                nc.vector.tensor_scalar(stat[:, 1, :], stat[:, 0, :], 1.0 / F, EPS_NORM, ALU.mult,
                                        ALU.add).then_inc(s_norm, 1)
                dve.wait_ge(s_nroot, g + 1)
                nc.vector.reciprocal(stat[:, 3, :], stat[:, 2, :]).then_inc(s_norm, 1)
                dve.wait_ge(s_norm, g * 8 + 8)
                nc.vector.tensor_tensor(out3, out3, stat[:, 3, :].unsqueeze(2).to_broadcast([P, PER, F]),
                                        ALU.mult).then_inc(s_done, 1)

            dve.wait_ge(s_added, PROD2 + EARLY * SUPERS)
            late_sums(0, 0, 0)
            totals(0)
            late_sums(1, 0, 1)
            finish(0, 0, 0)
            totals(1)
            with dve.Fori(1, SUPERS // 2) as q:
                late_sums(q * 2, q, 0)
                finish(q * 2 - 1, q - 1, 1)
                totals(q * 2)
                late_sums(q * 2 + 1, q, 1)
                finish(q * 2, q, 0)
                totals(q * 2 + 1)
            finish(SUPERS - 1, SUPERS // 2 - 1, 1)

        @block.tensor
        def _(pe):
            def half_product(m, tile, h, stationary, moving, start, stop):
                pe.wait_ge(s_tile[h], tile * 16 + 16)
                for b in range(HALF):
                    for c in range(SB // BANK):
                        last = nc.tensor.matmul(
                            prod_ps[:, ds((m % 2) * SB + c * BANK, BANK)], stationary(b),
                            moving(b * SB + c * BANK), start=start and b == 0, stop=stop and b == HALF - 1)
                last.then_inc(s_prod_half, 1)

            def product(number, tile, between=None):
                m, before, halves = number
                if not (isinstance(m, int) and m < 2):
                    pe.wait_ge(s_added, before)
                for h in range(2):
                    pe.wait_ge(s_staged, halves + h + 1)
                    half_product(m, tile, h, lambda b: y_stage[:, h, b * F:(b + 1) * F],
                                 lambda at: ring_slot(tile, h, at, BANK),
                                 h == 0, h == 1)
                    if h == 0 and between is not None:
                        between()

            def row_sums(ii):
                pe.wait_ge(s_acc, ii * (2 * SUPERS) + 2 * SUPERS)
                if not (isinstance(ii, int) and ii == 0):
                    pe.wait_ge(s_d, ii * 2)
                for b in range(PER):
                    last = nc.tensor.matmul(sums_ps[:, b:b + 1], acc[:, b * P:(b + 1) * P], ones[:, :],
                                            start=True, stop=True)
                last.then_inc(s_sums, 1)

            pe.wait_ge(s_memset, 4)
            pe.wait_ge(s_const, 64)
            def transpose_d():
                pe.wait_ge(s_d, 2 * SUPERS)
                nc.tensor.matmul(rows_ps, d1[:, :], ident[:, :], start=True, stop=True).then_inc(s_dall, 1)

            def row(ii, longer, within):
                if longer:
                    with pe.Fori(0, ii - 1) as gg:
                        product(low_product(ii, gg), lower_tile(ii, gg))
                product(low_product(ii, ii - 1), lower_tile(ii, ii - 1), (lambda: row_sums(ii)) if within else None)
                if not within:
                    row_sums(ii)
                if isinstance(ii, int) and ii == SUPERS - 1:
                    transpose_d()
                product(low_product(ii, ii), lower_tile(ii, ii))

            row_sums(0)
            product(low_product(0, 0), lower_tile(0, 0))
            row(1, False, False)
            with pe.Fori(2, LATE_ROW) as ii:
                row(ii, True, False)
            for ii in range(LATE_ROW, SUPERS):
                row(ii, True, True)

            def first_layer(k):
                pe.wait_ge(s_lap, k + 1)
                if not (isinstance(k, int) and k == 0):
                    pe.wait_ge(s_prez, k)
                else:
                    pe.wait_ge(s_drows, 1)
                for c in range(SB // BANK):
                    last = nc.tensor.matmul(z_ps[:, c * BANK:(c + 1) * BANK], w1[:, :],
                                            lap_t[:, c * BANK:(c + 1) * BANK], start=True, stop=True)
                last.then_inc(s_zps, 1)

            def squares(k):
                pe.wait_ge(s_zsq, k + 1)
                if not (isinstance(k, int) and k == 0):
                    pe.wait_ge(s_sq, k)
                for b in range(PER):
                    last = nc.tensor.matmul(sums_ps[:, b:b + 1], z_sq[:, b * P:(b + 1) * P], ones[:, :],
                                            start=True, stop=True)
                last.then_inc(s_sqps, 1)

            def high(k, j):
                m, before, _ = high_product(k, j)
                pe.wait_ge(s_added, before)
                for h in range(2):
                    v = high_half(k, j, h)
                    passes = ((y_stage_h, upper_slot, s_staged, 2 * LOW), (y_stage_l, upper_slot, s_ylow, 0),
                              (y_stage_h, lower_slot, s_lower, 0))
                    for i, (still, moving, ready, earlier) in enumerate(passes):
                        if i == 0:
                            pe.wait_ge(s_upper, v + 1)
                        pe.wait_ge(ready, v + (earlier + 1))
                        for b in range(HALF):
                            for c in range(SB // BANK):
                                last = nc.tensor.matmul(
                                    prod_ps[:, ds((m % 2) * SB + c * BANK, BANK)], still[:, h, b * F:(b + 1) * F],
                                    moving(v, b * SB + c * BANK, BANK),
                                    start=h == 0 and i == 0 and b == 0, stop=h == 1 and i == 2 and b == HALF - 1)
                        if i == 1:
                            last.then_inc(s_upper_used, 1)
                    last.then_inc(s_prod_half, 1)

            high(1, 0)
            first_layer(0)
            high(2, 0)
            squares(0)
            first_layer(1)
            high(2, 1)
            squares(1)
            with pe.Fori(3, SUPERS) as k:
                high(k, 0)
                first_layer(k - 1)
                with pe.Fori(1, k) as j:
                    high(k, j)
                squares(k - 1)
            first_layer(SUPERS - 1)
            squares(SUPERS - 1)
            pe.wait_ge(s_sq, SUPERS)
            nc.tensor.matmul(rows_ps, sq[:, :], ident[:, :], start=True, stop=True).then_inc(s_sqt, 1)

            def search(t, p, first=False, w=None):
                pe.wait_ge(s_zst, t + 1)
                for c in range(PER):
                    if not (first and c < 2):
                        pe.wait_ge(s_evac, t * PER + c - 1)
                    for half in range(SB // BANK):
                        n = c * (SB // BANK) + half
                        grp = 32 * (n % 4)
                        nc.tensor.matmul(score_ps[:, (c % 2) * SB + half * BANK:(c % 2) * SB + (half + 1) * BANK],
                                         ones_bf[grp:grp + 3, :],
                                         neg_half_sq[grp:grp + 3, (n // 4) * BANK:(n // 4 + 1) * BANK],
                                         start=True, stop=False)
                    for i, (still, moving) in enumerate(((z_stage_h, z_h), (z_stage_h, z_l), (z_stage_l, z_h))):
                        for half in range(SB // BANK):
                            n = c * (SB // BANK) + half
                            last = nc.tensor.matmul(
                                score_ps[:, (c % 2) * SB + half * BANK:(c % 2) * SB + (half + 1) * BANK],
                                still[:, p, :], moving[:, n * BANK:(n + 1) * BANK], start=False, stop=(i == 2))
                    last.then_inc(s_chunk, 1)
                    if w is not None:
                        piece(w, p, c)

            def piece(w, h, i):
                u, b, c = w // 2, i // 2, i % 2
                if i == 0:
                    if h == 0:
                        pe.wait_ge(s_added, u + (PROD2 - 1))
                    pe.wait_ge(s_y2l, (w // PERIOD) * 2 + h + 1)
                pe.wait_ge(s_lpiece, w * PIECES + i + 1)
                for n, (still, moving) in enumerate((
                        (y2_h, upper_pieces[i % 4][:, :]), (y2_l, upper_pieces[i % 4][:, :]),
                        (y2_h, lower_quarters[:, b, c * BANK:(c + 1) * BANK]))):
                    last = nc.tensor.matmul(prod_ps[:, ds(((u + PROD2) % 2) * SB + c * BANK, BANK)],
                                            still[:, h, b * F:(b + 1) * F], moving,
                                            start=h == 0 and b == 0 and n == 0,
                                            stop=h == 1 and b == HALF - 1 and n == 2)
                last.then_inc(s_piece, 1)

            def late_follow(pair, h):
                m = pair + (PROD2 - LAG // 2)
                if h == 0:
                    pe.wait_ge(s_added, m - 1)
                half_product(m, m + TILE_LATE, h, lambda b: y2_now[:, h, b * F:(b + 1) * F],
                             lambda at: late_ring[:, ds((m % 2) * (2 * HCOLS) + h * HCOLS + at, BANK)],
                             h == 0, h == 1)

            pe.wait_ge(s_split, 1)
            pe.wait_ge(s_sqld, 64)
            search(0, 0, True)
            search(1, 1)
            with pe.Fori(1, LAG // 2) as q:
                for p in range(2):
                    search(q * 2 + p, p)
            with pe.Fori(LAG // 2, BLOCKS // 2) as q:
                for p in range(2):
                    search(q * 2 + p, p, w=q * 2 + (p - LAG))
            pe.wait_ge(s_y2now[0], 16 * (EARLY + 1))
            with pe.Fori(BLOCKS // 2, EARLY * SUPERS + LAG // 2) as q:
                for p in range(2):
                    late_follow(q, p)

            def turn(g):
                pe.wait_ge(s_nsum, g + 1)
                if not (isinstance(g, int) and g == 0):
                    pe.wait_ge(s_tot, g)
                for b in range(PER):
                    last = nc.tensor.matmul(turned_ps[:, b * P:(b + 1) * P], near_sum[:, b * F:(b + 1) * F],
                                            ident[:, :], start=True, stop=True)
                last.then_inc(s_turn, 1)

            def dense(g):
                pe.wait_ge(s_tot, g + 1)
                if not (isinstance(g, int) and g == 0):
                    pe.wait_ge(s_norm, g * 8 - 6)
                for b in range(PER):
                    last = nc.tensor.matmul(dense_ps[:, b * F:(b + 1) * F], total_t[:, b * P:(b + 1) * P],
                                            w2[:, :], start=True, stop=True)
                last.then_inc(s_dense, 1)

            def late_products(ii, after_first):
                pe.wait_ge(s_added, ii + (PROD2 + EARLY * SUPERS - 1))
                for j in range(LATE):
                    m = ii * LATE + j + (PROD2 + EARLY * SUPERS)
                    for h in range(2):
                        half_product(ii, m + TILE_LATE, h,
                                     lambda b: y2_late[:, j * SB + (h * HALF + b) * F:j * SB + (h * HALF + b + 1) * F],
                                     lambda at: late_ring[:, (j % 2 * 2 + h) * HCOLS + at:(j % 2 * 2 + h) * HCOLS + at + BANK],
                                     j == 0 and h == 0, j == LATE - 1 and h == 1)
                    if j == 0 and after_first:
                        dense(ii - 1)
                turn(ii)

            pe.wait_ge(s_y2late, 16)
            late_products(0, False)
            late_products(1, True)
            with pe.Fori(2, SUPERS) as ii:
                late_products(ii, True)
            dense(SUPERS - 1)


def kernel(x, adj, L0_gnn_W1, L0_gnn_b1, L0_gnn_W2, L0_gnn_b2):
    import numpy as np
    import concourse.bacc as bacc
    from concourse import mybir as _mybir
    from concourse.bass_utils import run_bass_kernel_spmd as run

    x, adj = np.asarray(x), np.asarray(adj)
    n, f = x.shape
    p, sb = 128, 1024
    supers, half = n // sb, sb // p // 2
    x_part = np.ascontiguousarray(x.reshape(n // p, p, f).transpose(1, 0, 2)).reshape(p, n // p * f)
    tiles = np.ascontiguousarray(adj.reshape(supers, sb, supers, 2, half, p).transpose(0, 2, 3, 5, 4, 1))
    tiles = tiles.reshape(supers * supers * 2, p, half * sb)
    arrays = {"x_part": x_part, "adj_tiles": tiles, "w1_dram": np.ascontiguousarray(L0_gnn_W1),
              "b1_dram": np.ascontiguousarray(L0_gnn_b1), "w2_dram": np.ascontiguousarray(L0_gnn_W2),
              "b2_dram": np.ascontiguousarray(L0_gnn_b2)}
    nc = bacc.Bacc("TRN2", target_bir_lowering=False, num_devices=1)
    args = [nc.dram_tensor(k, a.shape, _mybir.dt.from_np(a.dtype), kind="ExternalInput").ap()
            for k, a in arrays.items()]
    out = nc.dram_tensor("out", (p, n // p * f), _mybir.dt.float32, kind="ExternalOutput").ap()
    resnorm_graph_kernel(nc, *args, out)
    r = run(nc, [arrays], core_ids=[0])
    got = np.asarray(r.results[0]["out"])
    return np.ascontiguousarray(got.reshape(p, n // p, f).transpose(1, 0, 2)).reshape(n, f)
```
